# Optimizing a Trainium2 kernel written in Bass

```python
import numpy as np
import jax
import jax.numpy as jnp

def _softmax(x, axis=-1):
    return jax.nn.softmax(x, axis=axis)

def _gelu(x):
    return jax.nn.gelu(x, approximate=True)

def _silu(x):
    return jax.nn.silu(x)

def _sigmoid(x):
    return jax.nn.sigmoid(x)

def _layernorm(x, axis=-1, eps=1e-05):
    m = jnp.mean(x, axis=axis, keepdims=True)
    v = jnp.var(x, axis=axis, keepdims=True)
    return (x - m) / jnp.sqrt(v + eps)

def _scatter_add(tgt, idx, src, axis=0):
    return tgt.at[idx].add(src)

def _segment_sum(src, seg, n):
    return jax.ops.segment_sum(src, seg, n)
kernel_name = 'mk_gnn_resnorm_d4_gnn_r32_725666'

def setup_inputs(seed: int=0):
    np.random.seed(seed)
    _w = jnp.asarray

    def _rec_inputs():
        import jax
        import jax.numpy as jnp
        _gk = jax.random.key(seed)
        x = -0.0003713 + 1 * jax.random.normal(jax.random.fold_in(_gk, 1), (3125, 128), jnp.float32)
        _s = jax.random.randint(jax.random.fold_in(_gk, 2), (25000,), 0, 3125, jnp.int32)
        _d = jax.random.randint(jax.random.fold_in(_gk, 3), (25000,), 0, 3125, jnp.int32)
        _loop = jnp.arange(3125, dtype=jnp.int32)
        src = jnp.concatenate([_s, _d, _loop])
        dst = jnp.concatenate([_d, _s, _loop])
        _o = jnp.argsort(dst, stable=True)
        src = src[_o]
        dst = dst[_o]
        edge_attr_128 = 0.00013283 + 1.0001 * jax.random.normal(jax.random.fold_in(_gk, 11), (53125, 128), jnp.float32)
        edge_weight1 = jax.random.uniform(jax.random.fold_in(_gk, 14), (53125, 1), jnp.float32, 0.0, 0.999998)
        return (x, src, dst, edge_attr_128, edge_weight1)
    x, src, dst, edge_attr_128, edge_weight1 = _rec_inputs()

    def _L0_gnn_setup():
        import jax, jax.numpy as jnp
        import numpy as np
        N = 3125
        E = 12500
        NFEAT, NHID, NOUT, NHEAD = (128, 64, 128, 4)
        HIDDEN = NHID * NHEAD
        SLOPE = 0.2

        def gat_conv(x, src, dst, W, a_src, a_dst, b, concat):
            H, C = a_src.shape
            h = (x @ W).reshape(N, H, C)
            al_s = (h * a_src).sum(-1)
            al_d = (h * a_dst).sum(-1)
            e = jax.nn.leaky_relu(al_s[src] + al_d[dst], SLOPE)
            m = jax.ops.segment_max(e, dst, num_segments=N)
            m = jnp.where(jnp.isfinite(m), m, 0.0)
            ex = jnp.exp(e - m[dst])
            denom = jax.ops.segment_sum(ex, dst, num_segments=N)
            alpha = ex / (denom[dst] + 1e-16)
            msg = alpha[:, :, None] * h[src]
            out = jax.ops.segment_sum(msg, dst, num_segments=N)
            out = out.reshape(N, H * C) if concat else out.mean(axis=1)
            return out + b
        key = jax.random.key(seed)
        ks = jax.random.split(key, 16)
        x = jax.random.normal(ks[0], (N, NFEAT), dtype=jnp.float32)
        edge_index = jax.random.randint(ks[1], (2, E), 0, N, dtype=jnp.int64)
        s = 0.1
        inp = {'x': x, 'edge_index': edge_index, 'W0': jax.random.normal(ks[2], (NFEAT, HIDDEN), jnp.float32) * s, 'as0': jax.random.normal(ks[3], (NHEAD, NHID), jnp.float32) * s, 'ad0': jax.random.normal(ks[4], (NHEAD, NHID), jnp.float32) * s, 'b0': jnp.zeros((HIDDEN,), jnp.float32), 'W1': jax.random.normal(ks[5], (HIDDEN, HIDDEN), jnp.float32) * s, 'as1': jax.random.normal(ks[6], (NHEAD, NHID), jnp.float32) * s, 'ad1': jax.random.normal(ks[7], (NHEAD, NHID), jnp.float32) * s, 'b1': jnp.zeros((HIDDEN,), jnp.float32), 'W2': jax.random.normal(ks[8], (HIDDEN, NOUT), jnp.float32) * s, 'as2': jax.random.normal(ks[9], (1, NOUT), jnp.float32) * s, 'ad2': jax.random.normal(ks[10], (1, NOUT), jnp.float32) * s, 'b2': jnp.zeros((NOUT,), jnp.float32)}
        return inp
    _L0_gnn_all = _L0_gnn_setup()
    _L0_gnn_in = {k: v for k, v in _L0_gnn_all.items() if k in ('W0', 'as0', 'ad0', 'b0', 'W1', 'as1', 'ad1', 'b1', 'W2', 'as2', 'ad2', 'b2')}
    del _L0_gnn_all

    def _L1_gnn_setup():
        import jax, jax.numpy as jnp
        import numpy as np
        N = 50000
        E = 50000
        IN_C = 128
        HID = 128
        HEADS = 4
        F_OUT = HID // HEADS
        NEG_SLOPE = 0.2

        def _glorot(key, shape):
            fan_in, fan_out = (shape[0], shape[-1])
            lim = jnp.sqrt(6.0 / (fan_in + fan_out)).astype(jnp.float32)
            return jax.random.uniform(key, shape, jnp.float32, -lim, lim)

        def gat_conv(x, src, dst, W, att_src, att_dst, b):
            n = x.shape[0]
            h = (x @ W).reshape(n, HEADS, F_OUT)
            a_s = jnp.einsum('nhf,hf->nh', h, att_src)
            a_d = jnp.einsum('nhf,hf->nh', h, att_dst)
            e = jax.nn.leaky_relu(a_s[src] + a_d[dst], NEG_SLOPE)
            e_max = jax.ops.segment_max(e, dst, num_segments=n)
            e_exp = jnp.exp(e - e_max[dst])
            denom = jax.ops.segment_sum(e_exp, dst, num_segments=n)
            denom = jnp.where(denom > 0, denom, 1.0)
            alpha = e_exp / denom[dst]
            msg = alpha[:, :, None] * h[src]
            out = jax.ops.segment_sum(msg, dst, num_segments=n)
            return out.reshape(n, HEADS * F_OUT) + b
        key = jax.random.key(seed)
        ks = jax.random.split(key, 12)
        x = jax.random.normal(ks[0], (N, IN_C), jnp.float32)
        edge_index = jax.random.randint(ks[1], (2, E), 0, N, jnp.int32)
        W0 = _glorot(ks[2], (IN_C, HEADS * F_OUT))
        att_src0 = _glorot(ks[3], (HEADS, F_OUT))
        att_dst0 = _glorot(ks[4], (HEADS, F_OUT))
        b0 = jnp.zeros((HEADS * F_OUT,), jnp.float32)
        W1 = _glorot(ks[5], (HID, HEADS * F_OUT))
        att_src1 = _glorot(ks[6], (HEADS, F_OUT))
        att_dst1 = _glorot(ks[7], (HEADS, F_OUT))
        b1 = jnp.zeros((HEADS * F_OUT,), jnp.float32)
        return {'x': x, 'edge_index': edge_index, 'W0': W0, 'att_src0': att_src0, 'att_dst0': att_dst0, 'b0': b0, 'W1': W1, 'att_src1': att_src1, 'att_dst1': att_dst1, 'b1': b1}
    _L1_gnn_all = _L1_gnn_setup()
    _L1_gnn_in = {k: v for k, v in _L1_gnn_all.items() if k in ('W0', 'att_src0', 'att_dst0', 'b0', 'W1', 'att_src1', 'att_dst1', 'b1')}
    del _L1_gnn_all

    def _L2_gnn_setup():
        import jax, jax.numpy as jnp
        import numpy as np
        N_NODES = 3125
        N_EDGES = 18750
        D = 128
        DE = 128
        EPS_LN = 1e-05
        EPS_SM = 1e-16
        key = jax.random.key(seed)
        ks = jax.random.split(key, 12)
        x = jax.random.normal(ks[0], (N_NODES, D), jnp.float32)
        edge_index = jax.random.randint(ks[1], (2, N_EDGES), 0, N_NODES, dtype=jnp.int64)
        edge_type = jax.random.uniform(ks[2], (N_EDGES, 1), jnp.float32)
        edge_vector = jax.random.normal(ks[3], (N_EDGES, DE), jnp.float32)
        s_t = 1.0 / np.sqrt(D + DE)
        s = 1.0 / np.sqrt(D)
        Wt = jax.random.normal(ks[4], (D + DE, D), jnp.float32) * s_t
        bt = jnp.zeros((D,), jnp.float32)
        Wq = jax.random.normal(ks[5], (D, D), jnp.float32) * s
        bq = jnp.zeros((D,), jnp.float32)
        Wk = jax.random.normal(ks[6], (D, D), jnp.float32) * s
        bk = jnp.zeros((D,), jnp.float32)
        Wv = jax.random.normal(ks[7], (D, D), jnp.float32) * s
        bv = jnp.zeros((D,), jnp.float32)
        gamma = jnp.ones((D,), jnp.float32)
        beta = jnp.zeros((D,), jnp.float32)
        return {'x': x, 'edge_index': edge_index, 'edge_type': edge_type, 'edge_vector': edge_vector, 'gamma': gamma, 'beta': beta, 'Wt': Wt, 'bt': bt, 'Wq': Wq, 'bq': bq, 'Wk': Wk, 'bk': bk, 'Wv': Wv, 'bv': bv}
    _L2_gnn_all = _L2_gnn_setup()
    _L2_gnn_in = {k: v for k, v in _L2_gnn_all.items() if k in ('gamma', 'beta', 'Wt', 'bt', 'Wq', 'bq', 'Wk', 'bk', 'Wv', 'bv')}
    del _L2_gnn_all

    def _L3_gnn_setup():
        import jax, jax.numpy as jnp
        import numpy as np
        N_NODES = 50000
        N_EDGES = 18750
        D = 128
        key = jax.random.key(seed)
        ks = jax.random.split(key, 6)
        node_features = jax.random.normal(ks[0], (N_NODES, D), dtype=jnp.float32)
        edge_index = jax.random.randint(ks[1], (N_EDGES, 2), 0, N_NODES, dtype=jnp.int64)
        scale = 1.0 / np.sqrt(D)
        W1 = jax.random.uniform(ks[2], (D, D), jnp.float32, -scale, scale)
        b1 = jax.random.uniform(ks[3], (D,), jnp.float32, -scale, scale)
        W2 = jax.random.uniform(ks[4], (D, D), jnp.float32, -scale, scale)
        b2 = jax.random.uniform(ks[5], (D,), jnp.float32, -scale, scale)
        return {'node_features': node_features, 'edge_index': edge_index, 'W1': W1, 'b1': b1, 'W2': W2, 'b2': b2}
    _L3_gnn_all = _L3_gnn_setup()
    _L3_gnn_in = {k: v for k, v in _L3_gnn_all.items() if k in ('W1', 'b1', 'W2', 'b2')}
    del _L3_gnn_all
    return {'x': x, 'src': src, 'dst': dst, 'edge_attr_128': edge_attr_128, 'edge_weight1': edge_weight1, 'L0_gnn_W0': _L0_gnn_in['W0'], 'L0_gnn_as0': _L0_gnn_in['as0'], 'L0_gnn_ad0': _L0_gnn_in['ad0'], 'L0_gnn_b0': _L0_gnn_in['b0'], 'L0_gnn_W1': _L0_gnn_in['W1'], 'L0_gnn_as1': _L0_gnn_in['as1'], 'L0_gnn_ad1': _L0_gnn_in['ad1'], 'L0_gnn_b1': _L0_gnn_in['b1'], 'L0_gnn_W2': _L0_gnn_in['W2'], 'L0_gnn_as2': _L0_gnn_in['as2'], 'L0_gnn_ad2': _L0_gnn_in['ad2'], 'L0_gnn_b2': _L0_gnn_in['b2'], 'L1_gnn_W0': _L1_gnn_in['W0'], 'L1_gnn_att_src0': _L1_gnn_in['att_src0'], 'L1_gnn_att_dst0': _L1_gnn_in['att_dst0'], 'L1_gnn_b0': _L1_gnn_in['b0'], 'L1_gnn_W1': _L1_gnn_in['W1'], 'L1_gnn_att_src1': _L1_gnn_in['att_src1'], 'L1_gnn_att_dst1': _L1_gnn_in['att_dst1'], 'L1_gnn_b1': _L1_gnn_in['b1'], 'L2_gnn_gamma': _L2_gnn_in['gamma'], 'L2_gnn_beta': _L2_gnn_in['beta'], 'L2_gnn_Wt': _L2_gnn_in['Wt'], 'L2_gnn_bt': _L2_gnn_in['bt'], 'L2_gnn_Wq': _L2_gnn_in['Wq'], 'L2_gnn_bq': _L2_gnn_in['bq'], 'L2_gnn_Wk': _L2_gnn_in['Wk'], 'L2_gnn_bk': _L2_gnn_in['bk'], 'L2_gnn_Wv': _L2_gnn_in['Wv'], 'L2_gnn_bv': _L2_gnn_in['bv'], 'L3_gnn_W1': _L3_gnn_in['W1'], 'L3_gnn_b1': _L3_gnn_in['b1'], 'L3_gnn_W2': _L3_gnn_in['W2'], 'L3_gnn_b2': _L3_gnn_in['b2']}

def reference(x, src, dst, edge_attr_128, edge_weight1, L0_gnn_W0, L0_gnn_as0, L0_gnn_ad0, L0_gnn_b0, L0_gnn_W1, L0_gnn_as1, L0_gnn_ad1, L0_gnn_b1, L0_gnn_W2, L0_gnn_as2, L0_gnn_ad2, L0_gnn_b2, L1_gnn_W0, L1_gnn_att_src0, L1_gnn_att_dst0, L1_gnn_b0, L1_gnn_W1, L1_gnn_att_src1, L1_gnn_att_dst1, L1_gnn_b1, L2_gnn_gamma, L2_gnn_beta, L2_gnn_Wt, L2_gnn_bt, L2_gnn_Wq, L2_gnn_bq, L2_gnn_Wk, L2_gnn_bk, L2_gnn_Wv, L2_gnn_bv, L3_gnn_W1, L3_gnn_b1, L3_gnn_W2, L3_gnn_b2):
    import jax
    import jax.numpy as jnp

    def _L0_gnn_ref(x, edge_index, W0, as0, ad0, b0, W1, as1, ad1, b1, W2, as2, ad2, b2):
        import jax, jax.numpy as jnp
        import numpy as np
        N = 3125
        E = 12500
        NFEAT, NHID, NOUT, NHEAD = (128, 64, 128, 4)
        HIDDEN = NHID * NHEAD
        SLOPE = 0.2

        def gat_conv(x, src, dst, W, a_src, a_dst, b, concat):
            H, C = a_src.shape
            h = (x @ W).reshape(N, H, C)
            al_s = (h * a_src).sum(-1)
            al_d = (h * a_dst).sum(-1)
            e = jax.nn.leaky_relu(al_s[src] + al_d[dst], SLOPE)
            m = jax.ops.segment_max(e, dst, num_segments=N)
            m = jnp.where(jnp.isfinite(m), m, 0.0)
            ex = jnp.exp(e - m[dst])
            denom = jax.ops.segment_sum(ex, dst, num_segments=N)
            alpha = ex / (denom[dst] + 1e-16)
            msg = alpha[:, :, None] * h[src]
            out = jax.ops.segment_sum(msg, dst, num_segments=N)
            out = out.reshape(N, H * C) if concat else out.mean(axis=1)
            return out + b
        loop = jnp.arange(N, dtype=edge_index.dtype)
        src = jnp.concatenate([edge_index[0], loop])
        dst = jnp.concatenate([edge_index[1], loop])
        h = jax.nn.elu(gat_conv(x, src, dst, W0, as0, ad0, b0, concat=True))
        h = jax.nn.elu(gat_conv(h, src, dst, W1, as1, ad1, b1, concat=True))
        out = gat_conv(h, src, dst, W2, as2, ad2, b2, concat=False)
        return out

    def _L1_gnn_ref(x, edge_index, W0, att_src0, att_dst0, b0, W1, att_src1, att_dst1, b1):
        import jax, jax.numpy as jnp
        import numpy as np
        N = 50000
        E = 50000
        IN_C = 128
        HID = 128
        HEADS = 4
        F_OUT = HID // HEADS
        NEG_SLOPE = 0.2

        def _glorot(key, shape):
            fan_in, fan_out = (shape[0], shape[-1])
            lim = jnp.sqrt(6.0 / (fan_in + fan_out)).astype(jnp.float32)
            return jax.random.uniform(key, shape, jnp.float32, -lim, lim)

        def gat_conv(x, src, dst, W, att_src, att_dst, b):
            n = x.shape[0]
            h = (x @ W).reshape(n, HEADS, F_OUT)
            a_s = jnp.einsum('nhf,hf->nh', h, att_src)
            a_d = jnp.einsum('nhf,hf->nh', h, att_dst)
            e = jax.nn.leaky_relu(a_s[src] + a_d[dst], NEG_SLOPE)
            e_max = jax.ops.segment_max(e, dst, num_segments=n)
            e_exp = jnp.exp(e - e_max[dst])
            denom = jax.ops.segment_sum(e_exp, dst, num_segments=n)
            denom = jnp.where(denom > 0, denom, 1.0)
            alpha = e_exp / denom[dst]
            msg = alpha[:, :, None] * h[src]
            out = jax.ops.segment_sum(msg, dst, num_segments=n)
            return out.reshape(n, HEADS * F_OUT) + b
        src, dst = (edge_index[0], edge_index[1])
        h = gat_conv(x, src, dst, W0, att_src0, att_dst0, b0)
        h = jax.nn.relu(h)
        out = gat_conv(h, src, dst, W1, att_src1, att_dst1, b1)
        return out

    def _L2_gnn_ref(x, edge_index, edge_type, edge_vector, gamma, beta, Wt, bt, Wq, bq, Wk, bk, Wv, bv):
        import jax, jax.numpy as jnp
        import numpy as np
        N_NODES = 3125
        N_EDGES = 18750
        D = 128
        DE = 128
        EPS_LN = 1e-05
        EPS_SM = 1e-16
        d_sqrt = jnp.sqrt(jnp.asarray(D, x.dtype))
        residual = x
        mu = jnp.mean(x, axis=-1, keepdims=True)
        var = jnp.var(x, axis=-1, keepdims=True)
        h = (x - mu) / jnp.sqrt(var + EPS_LN) * gamma + beta
        src, dst = (edge_index[0], edge_index[1])
        x_j = h[src]
        x_i = h[dst]
        t = jax.nn.gelu(jnp.concatenate([x_j, edge_vector], axis=1) @ Wt + bt, approximate=False)
        q = x_i @ Wq + bq
        k = t @ Wk + bk
        attn = jnp.sum(k * q, axis=-1, keepdims=True)
        attn = attn * edge_type / d_sqrt
        m = jax.ops.segment_max(attn, dst, num_segments=N_NODES)
        e = jnp.exp(attn - m[dst])
        s = jax.ops.segment_sum(e, dst, num_segments=N_NODES)
        a = e / (s[dst] + EPS_SM)
        msg = a * (t @ Wv + bv)
        aggr = jax.ops.segment_sum(msg, dst, num_segments=N_NODES)
        return residual + jax.nn.gelu(aggr, approximate=False)

    def _L3_gnn_ref(node_features, edge_index, W1, b1, W2, b2):
        import jax, jax.numpy as jnp
        import numpy as np
        N_NODES = 50000
        N_EDGES = 18750
        D = 128
        src = edge_index[:, 0]
        tgt = edge_index[:, 1]
        messages = jax.nn.relu(node_features[src] @ W1.T + b1)
        agg = jax.ops.segment_sum(messages, tgt, num_segments=node_features.shape[0])
        return jax.nn.relu((agg + node_features) @ W2.T + b2)
    edge_index = jnp.stack([src, dst])
    edge_index_t = jnp.stack([src, dst], axis=1)
    x = _layernorm(x + _L0_gnn_ref(x, edge_index, L0_gnn_W0, L0_gnn_as0, L0_gnn_ad0, L0_gnn_b0, L0_gnn_W1, L0_gnn_as1, L0_gnn_ad1, L0_gnn_b1, L0_gnn_W2, L0_gnn_as2, L0_gnn_ad2, L0_gnn_b2), axis=-1)
    x = _layernorm(x + _L1_gnn_ref(x, edge_index, L1_gnn_W0, L1_gnn_att_src0, L1_gnn_att_dst0, L1_gnn_b0, L1_gnn_W1, L1_gnn_att_src1, L1_gnn_att_dst1, L1_gnn_b1), axis=-1)
    x = _layernorm(x + _L2_gnn_ref(x, edge_index, edge_weight1, edge_attr_128, L2_gnn_gamma, L2_gnn_beta, L2_gnn_Wt, L2_gnn_bt, L2_gnn_Wq, L2_gnn_bq, L2_gnn_Wk, L2_gnn_bk, L2_gnn_Wv, L2_gnn_bv), axis=-1)
    x = _layernorm(x + _L3_gnn_ref(x, edge_index_t, L3_gnn_W1, L3_gnn_b1, L3_gnn_W2, L3_gnn_b2), axis=-1)
    return x

_drawn_inputs = setup_inputs


def setup_inputs(seed=0):
    import zlib

    import numpy as np

    out = dict(_drawn_inputs(seed))
    spreads = {'L0_gnn_b0': (0.0, 0.1),
     'L0_gnn_b1': (0.0, 0.1),
     'L0_gnn_b2': (0.0, 0.1),
     'L1_gnn_b0': (0.0, 0.1),
     'L1_gnn_b1': (0.0, 0.1),
     'L2_gnn_gamma': (1.0, 0.6),
     'L2_gnn_beta': (0.0, 0.552),
     'L2_gnn_bt': (0.0, 0.515),
     'L2_gnn_bq': (0.0, 0.8),
     'L2_gnn_bk': (0.0, 0.8),
     'L2_gnn_bv': (0.0, 0.1)}
    factors = {'edge_weight1': 8.0,
     'L0_gnn_ad0': 5.072,
     'L0_gnn_ad1': 8.0,
     'L0_gnn_as2': 5.263,
     'L0_gnn_ad2': 8.0,
     'L1_gnn_att_dst0': 3.314,
     'L1_gnn_att_src1': 3.095,
     'L1_gnn_att_dst1': 7.993,
     'L2_gnn_Wq': 4.312,
     'L2_gnn_Wk': 4.539}
    for name, (base, spread) in spreads.items():
        noise = np.random.default_rng([zlib.crc32(name.encode()), seed]).standard_normal(out[name].shape)
        drawn = base * np.exp(spread * noise) if base else spread * noise
        out[name] = jnp.asarray(drawn.astype(out[name].dtype))
    for name, factor in factors.items():
        out[name] = (out[name] * factor).astype(out[name].dtype)
    return out
```

```python
import concourse.bass as bass
from concourse import mybir
from contextlib import ExitStack

f32 = mybir.dt.float32
bf16 = mybir.dt.bfloat16
i32 = mybir.dt.int32
u32 = mybir.dt.uint32
ALU = mybir.AluOpType
ACT = mybir.ActivationFunctionType
AX = mybir.AxisListType
ds = bass.ds

N = 3125
E = 53125
P = 128
NB = -(-N // P)
LASTN = N - (NB - 1) * P
D = 128
TG = 2
GE = TG * P
NG = (E + NB * (GE - 1)) // GE
NT = NG * TG
EC = -(-E // P)
EFULL = E // EC
EREST = E - EFULL * EC
UN = 4
NEG = -1.0e30
SLOPE = 0.2
EPS_SM = 1e-16
EPS_LN = 1e-5
PEEL = 4
assert NG % UN == 0


def bc(ap, axis, n):
    a = ap.unsqueeze(axis)
    shape = list(a.shape)
    shape[axis] = n
    return a.to_broadcast(shape)


def rows(ap1d):
    return ap1d.partition_broadcast(P)


def pipeline(eng, step, last):
    for i in range(PEEL):
        step(i, i % UN)
    with eng.Fori(0, (NG - 2 * PEEL) // UN) as j:
        for r in range(UN):
            step(j * UN + (PEEL + r), (PEEL + r) % UN)
    for i in range(NG - PEEL, last):
        step(i, i % UN)


def gnn(nc, T, out, stop=None):
    ctx = ExitStack()
    sb = lambda n, s, d=f32: ctx.enter_context(nc.sbuf_tensor(n, s, d))
    sem = lambda n: ctx.enter_context(nc.semaphore(n))
    with ctx:
        ident = sb("ident", [P, P])
        identb = sb("identb", [P, P], bf16)
        neg_ident = sb("neg_ident", [P, P], bf16)
        iota_row = sb("iota_row", [P, P])
        ones = sb("ones", [P, P])
        tri = sb("tri", [P, P])
        head_sel = sb("head_sel", [12, 4, P], bf16)
        head_sel1 = sb("head_sel1", [3, 1, P], bf16)
        e_src = sb("e_src", [P, NT], u32)
        e_id = sb("e_id", [P, NT], u32)
        e_ld = sb("e_ld", [P, NT])
        e_w = sb("e_w", [P, NT])
        blk = sb("blk", [1, NG], i32)
        X = sb("X", [P, NB, D])
        Y = sb("Y", [P, NB, 256])
        Z = sb("Z", [P, NB, 266])
        acc = sb("acc", [P, NB, 260])
        QK = sb("QK", [P, NB, D + 1])
        V = sb("V", [P, NB, 8])
        small = sb("small", [P, 4, NB * 4])
        WA = sb("WA", [P, 2, 264])
        WR = sb("WR", [P, 2, 256])
        WT2 = sb("WT2", [P, D])
        vec = sb("vec", [P, 2, 256])
        brow = sb("brow", [P, 4, 256])
        wtmp = sb("wtmp", [P, 256])
        H = [sb(f"H{i}", [P, TG, 266]) for i in range(UN)]
        EV = [sb(f"EV{i}", [P, TG, D]) for i in range(UN)]
        idx = [sb(f"idx{i}", [P, 2, UN * TG], u32) for i in range(2)]
        O = [sb(f"O{i}", [P, TG, P]) for i in range(UN)]
        NE = [sb(f"NE{i}", [P, TG, P], bf16) for i in range(UN)]
        OT = [sb(f"OT{i}", [P, TG, P]) for i in range(UN)]
        asT = [sb(f"asT{i}", [12, TG, P], bf16) for i in range(2)]
        evT = [sb(f"evT{i}", [P, TG, P]) for i in range(2)]
        Hx = [sb(f"Hx{i}", [P, TG, 260]) for i in range(2)]
        Tt = [sb(f"Tt{i}", [P, TG, D]) for i in range(UN)]
        attn = [sb(f"attn{i}", [P, TG]) for i in range(UN)]
        z = [sb(f"z{i}", [P, TG, 4]) for i in range(UN)]
        gm = sb("gm", [P, 4])
        tm = sb("tm", [P, 4])
        mn = sb("mn", [P, 4])
        dm = [sb(f"dm{i}", [P, 4]) for i in range(UN)]
        sc = [sb(f"sc{i}", [P, 4]) for i in range(UN)]
        junk = sb("junk", [P, TG, D])
        pb = lambda n, s: ctx.enter_context(nc.psum_tensor(n, s, f32))
        psM = [pb(f"psM{i}", [P, TG, 512]) for i in range(2)]
        psT = pb("psT", [P, 512])
        psG = pb("psG", [P, 512])
        psS = [pb(f"psS{i}", [P, 512]) for i in range(2)]

        s_step = sem("s_step")
        s_load = sem("s_load")
        steps = [0]
        loads = [0]

        def link(eng, ins):
            steps[0] += 1
            ins.then_inc(s_step, 1)
            eng.wait_ge(s_step, steps[0])

        def load(eng, dst, src):
            loads[0] += 16
            eng.dma_start(dst, src).then_inc(s_load, 16)

        def loaded(eng):
            eng.wait_ge(s_load, loads[0])

        def setup():
            with ExitStack() as c2:
                sb2 = lambda n, s, d=f32: c2.enter_context(nc.sbuf_tensor(n, s, d))
                dst_i = sb2("dst_i", [P, EC], i32)
                src_i = sb2("src_i", [P, EC], i32)
                w_in = sb2("w_in", [P, EC])
                kb_i = sb2("kb_i", [P, EC], i32)
                ld_i = sb2("ld_i", [P, EC], i32)
                kb = sb2("kb", [P, EC])
                eq = sb2("eq", [P, EC])
                cnt = sb2("cnt", [P, EC])
                rank = sb2("rank", [P, EC])
                one_c = sb2("one_c", [P, EC])
                bid = sb2("bid", [P, NB])
                tot = sb2("tot", [P, NB])
                ngr = sb2("ngr", [P, 5, NB])
                ngi = sb2("ngi", [P, NB], i32)
                base = sb2("base", [P, NB])
                rec = sb2("rec", [P, EC, 4])
                pos = sb2("pos", [P, EC], i32)
                dest = sb2("dest", [P, EC], u32)
                jio = sb2("jio", [1, NG])
                jcmp = acc[0:1, :, :].rearrange("p b c -> p (b c)")[:, 0:NG * NB].rearrange("p (g b) -> p g b", g=NG)
                jblk = sb2("jblk", [1, NG])
                pad = Z[:, :, :].rearrange("p b c -> p (b c)")[:, 0:NT * 4].rearrange("p (t f) -> p t f", f=4)
                SC = 8
                rslot = [sb2(f"rslot{i}", [P, SC, 4]) for i in range(2)]
                dslot = [sb2(f"dslot{i}", [P, SC], u32) for i in range(2)]
                sorted_e = nc.dram_tensor("sorted_e", [P * NT, 4], f32).ap()
                s_const = sem("s_const")
                s_in = sem("s_in")
                s_eq = sem("s_eq"); s_cnt = sem("s_cnt"); s_mul = sem("s_mul"); s_rank = sem("s_rank")
                s_tot = sem("s_tot"); s_pre = sem("s_pre"); s_rec = sem("s_rec")
                s_padded = sem("s_padded")
                s_slot = sem("s_slot"); s_scat = [sem("s_scat0"), sem("s_scat1")]
                s_back = sem("s_back")
                s_pool = sem("s_pool")

                with nc.Block() as block:
                    @block.gpsimd
                    def _(g):
                        n = [0]

                        def own(ins):
                            n[0] += 1
                            ins.then_inc(s_pool, 1)
                            g.wait_ge(s_pool, n[0])
                        own(g.memset(dst_i[:, :], 99 * P))
                        own(g.memset(src_i[:, :], 0))
                        own(g.memset(w_in[:, :], 0.0))
                        for t, name in ((dst_i, "dst"), (src_i, "src"), (w_in, "edge_weight1")):
                            flat = T[name].rearrange("a b -> (a b)") if name == "edge_weight1" else T[name]
                            g.dma_start(t[0:EFULL, :], flat[0:EFULL * EC].rearrange("(p c) -> p c", c=EC)).then_inc(s_in, 16)
                            g.dma_start(t[EFULL:EFULL + 1, 0:EREST],
                                        flat[EFULL * EC:E].rearrange("(p c) -> p c", c=EREST)).then_inc(s_in, 16)
                        own(g.memset(ones[:, :], 1.0))
                        own(g.memset(ident[:, :], 0.0))
                        own(g.memset(head_sel[:, :, :], 1.0))
                        own(g.memset(head_sel1[:, :, :], 1.0))
                        own(g.affine_select(out=ident[:, :], in_=ident[:, :], compare_op=ALU.not_equal, fill=1.0,
                                            base=0, pattern=[[-1, P]], channel_multiplier=1))
                        own(g.affine_select(out=tri[:, :], in_=ones[:, :], compare_op=ALU.is_gt, fill=0.0,
                                            base=0, pattern=[[1, P]], channel_multiplier=-1))
                        own(g.affine_select(out=head_sel[:, :, :], in_=head_sel[:, :, :], compare_op=ALU.is_ge, fill=0.0,
                                            base=0, pattern=[[-3, 4], [0, P]], channel_multiplier=1))
                        own(g.affine_select(out=head_sel[:, :, :], in_=head_sel[:, :, :], compare_op=ALU.is_ge, fill=0.0,
                                            base=2, pattern=[[3, 4], [0, P]], channel_multiplier=-1))
                        own(g.iota(kb_i[:, 0:P], pattern=[[1, P]], base=0, channel_multiplier=0))
                        own(g.tensor_copy(iota_row[:, :], kb_i[:, 0:P]))
                        own(g.tensor_copy(bid[:, :], kb_i[:, 0:NB]))
                        own(g.iota(kb_i[0:1, 0:NG], pattern=[[1, NG]], base=0, channel_multiplier=0))
                        own(g.tensor_copy(jio[:, :], kb_i[0:1, 0:NG]))
                        own(g.iota(ld_i[:, :], pattern=[[1, EC]], base=0, channel_multiplier=EC))
                        own(g.tensor_copy(rec[:, :, 2], ld_i[:, :]))
                        own(g.memset(one_c[:, :], 1.0))
                        own(g.memset(pad[:, :, :], 0.0))
                        own(g.memset(pad[:, :, 1], 999.0))
                        g.sem_inc(s_const, 1)
                        g.dma_start(sorted_e.rearrange("(p t) f -> p t f", p=P), pad[:, :, :]).then_inc(s_padded, 16)
                        g.wait_ge(s_padded, 16)

                        def scatter(j, h, cols):
                            g.wait_ge(s_slot, j + 1)
                            g.sem_inc(s_pool, 1)
                            for k in range(cols):
                                g.indirect_dma_start(
                                    out=sorted_e[:, :], out_offset=bass.IndirectOffsetOnAxis(ap=dslot[h][:, k:k + 1], axis=0),
                                    in_=rslot[h][:, k, :], in_offset=None, bounds_check=P * NT - 1,
                                    oob_is_err=False).then_inc(s_scat[h], 16)
                        NS = EC // SC
                        assert EC % SC == 0 and NS % 2 == 0
                        with g.Fori(0, NS // 2) as j:
                            for h in range(2):
                                scatter(j * 2 + h, h, SC)
                        for h in range(2):
                            g.wait_ge(s_scat[h], NS // 2 * SC * 16)
                        g.dma_start(pad[:, :, :], sorted_e.rearrange("(p t) f -> p t f", p=P)).then_inc(s_back, 16)

                    @block.vector
                    def _(v):
                        v.wait_ge(s_const, 1)
                        v.wait_ge(s_in, 96)
                        link(v, v.tensor_copy(identb[:, :], ident[:, :]))
                        link(v, v.tensor_scalar(neg_ident[:, :], ident[:, :], NEG, None, ALU.mult))
                        link(v, v.tensor_scalar(kb_i[:, :], dst_i[:, :], 7, None, ALU.logical_shift_right))
                        link(v, v.tensor_scalar(ld_i[:, :], dst_i[:, :], P - 1, None, ALU.bitwise_and))
                        link(v, v.tensor_copy(kb[:, :], kb_i[:, :]))
                        link(v, v.tensor_copy(rec[:, :, 1], ld_i[:, :]))
                        link(v, v.tensor_copy(rec[:, :, 0], src_i[:, :]))
                        link(v, v.tensor_copy(rec[:, :, 3], w_in[:, :]))
                        link(v, v.memset(rank[:, :], 0.0))
                        with v.Fori(0, NB) as b:
                            v.tensor_scalar(eq[:, :], kb[:, :], bid[:, ds(b, 1)], None, ALU.is_equal).then_inc(s_eq, 1)
                            v.wait_ge(s_eq, b + 1)
                            v.tensor_tensor_scan(cnt[:, :], one_c[:, :], eq[:, :], 0.0, ALU.mult, ALU.add).then_inc(s_cnt, 1)
                            v.wait_ge(s_cnt, b + 1)
                            v.tensor_scalar(tot[:, ds(b, 1)], cnt[:, EC - 1:EC], 1.0, None, ALU.mult).then_inc(s_tot, 1)
                            v.tensor_tensor(eq[:, :], eq[:, :], cnt[:, :], ALU.mult).then_inc(s_mul, 1)
                            v.wait_ge(s_mul, b + 1)
                            v.tensor_tensor(rank[:, :], rank[:, :], eq[:, :], ALU.add).then_inc(s_rank, 1)
                            v.wait_ge(s_rank, b + 1)
                            v.wait_ge(s_tot, b + 1)
                        v.wait_ge(s_pre, 1)
                        pre, al = psG[:, 0:NB], psG[:, 64:64 + NB]
                        link(v, v.tensor_scalar(ngi[:, :], al, float(GE - 1), None, ALU.add))
                        link(v, v.tensor_scalar(kb_i[:, 0:NB], ngi[:, :], 8, None, ALU.logical_shift_right))
                        link(v, v.tensor_copy(ngr[:, 0, :], kb_i[:, 0:NB]))
                        gend = ngr[:, 1, :]
                        link(v, v.tensor_tensor_scan(gend, one_c[:, 0:NB], ngr[:, 0, :], 0.0, ALU.mult, ALU.add))
                        link(v, v.tensor_tensor(ngr[:, 2, :], gend, ngr[:, 0, :], ALU.subtract))
                        link(v, v.tensor_scalar(ngr[:, 3, :], ngr[:, 2, :], float(GE), -1.0, ALU.mult, ALU.add))
                        link(v, v.tensor_tensor(base[:, :], ngr[:, 3, :], pre, ALU.add))
                        with v.Fori(0, NB) as b:
                            v.tensor_scalar(eq[:, :], kb[:, :], bid[:, ds(b, 1)], base[:, ds(b, 1)],
                                            ALU.is_equal, ALU.mult).then_inc(s_eq, 1)
                            v.wait_ge(s_eq, b + (NB + 1))
                            v.tensor_tensor(rank[:, :], rank[:, :], eq[:, :], ALU.add).then_inc(s_rank, 1)
                            v.wait_ge(s_rank, b + (NB + 1))
                        link(v, v.tensor_copy(pos[:, :], rank[:, :]))
                        link(v, v.tensor_scalar(ld_i[:, :], pos[:, :], P - 1, None, ALU.bitwise_and))
                        link(v, v.tensor_scalar(kb_i[:, :], pos[:, :], 7, None, ALU.logical_shift_right))
                        link(v, v.tensor_copy(eq[:, :], ld_i[:, :]))
                        link(v, v.tensor_copy(cnt[:, :], kb_i[:, :]))
                        link(v, v.scalar_tensor_tensor(rank[:, :], eq[:, :], float(NT), cnt[:, :], ALU.mult, ALU.add))
                        link(v, v.tensor_scalar(eq[:, :], kb[:, :], float(NB), 1.0e6, ALU.is_ge, ALU.mult))
                        link(v, v.tensor_tensor(cnt[:, :], rank[:, :], eq[:, :], ALU.add))
                        link(v, v.tensor_scalar(cnt[:, :], cnt[:, :], 0.0, None, ALU.max))
                        link(v, v.tensor_copy(dest[:, :], cnt[:, :]))

                        def slots(j, h):
                            v.tensor_copy(rslot[h][:, :, :], rec[:, ds(j * SC, SC), :]).then_inc(s_mul, 1)
                            v.tensor_copy(dslot[h][:, :], dest[:, ds(j * SC, SC)]).then_inc(s_slot, 1)
                        for h in range(2):
                            slots(h, h)
                        with v.Fori(1, EC // SC // 2) as j:
                            for h in range(2):
                                v.wait_ge(s_scat[h], j * (SC * 16))
                                v.sem_inc(s_rec, 1)
                                slots(j * 2 + h, h)
                        link(v, v.tensor_tensor(jcmp[:, :, :], bc(jio[:, :], 2, NB), bc(gend[0:1, :], 1, NG), ALU.is_ge))
                        link(v, v.reduce_sum(jblk[:, :], jcmp[:, :, :], AX.X))
                        link(v, v.tensor_scalar(blk[:, :], jblk[:, :], float(NB - 1), None, ALU.min))
                        v.wait_ge(s_back, 16)
                        link(v, v.tensor_copy(e_src[:, :], pad[:, :, 0]))
                        link(v, v.tensor_copy(e_ld[:, :], pad[:, :, 1]))
                        link(v, v.tensor_copy(e_id[:, :], pad[:, :, 2]))
                        link(v, v.tensor_scalar(e_w[:, :], pad[:, :, 3], float(D) ** -0.5, None, ALU.mult))

                    @block.tensor
                    def _(pe):
                        pe.wait_ge(s_tot, NB)
                        pe.matmul(psG[:, 0:NB], tri[:, :], tot[:, :], start=True, stop=True)
                        pe.matmul(psG[:, 64:64 + NB], ones[:, :], tot[:, :], start=True, stop=True).then_inc(s_pre, 1)

        nm_in, nm_tr, nm_ev, nm_mm, nm_out = (sem(n) for n in ("nm_in", "nm_tr", "nm_ev", "nm_mm", "nm_out"))
        nm_base = [0]
        xs = [sb(f"xs{i}", [P, 256]) for i in range(2)]
        xT = [sb(f"xT{i}", [P, 2, P]) for i in range(2)]

        def node_matmul(src, K, W, cols, dst):
            kt = K // P
            B = nm_base[0]
            nm_base[0] += NB

            def blocks(eng, step):
                step(0, 0)
                step(1, 1)
                with eng.Fori(1, NB // 2) as j:
                    step(j * 2, 0)
                    step(j * 2 + 1, 1)
                for b in range(NB // 2 * 2, NB):
                    step(b, b % 2)

            def w(eng, s, b, back):
                if not (isinstance(b, int) and b < back):
                    eng.wait_ge(s, b + (B + 1 - back))

            with nc.Block() as block:
                @block.vector
                def _(v):
                    def step(b, s):
                        w(v, nm_tr, b, 2)
                        v.tensor_tensor(xs[s][:, 0:K], src[:, ds(b, 1), :].rearrange("p a k -> p (a k)"),
                                        src[:, ds(b, 1), :].rearrange("p a k -> p (a k)"), ALU.max).then_inc(nm_in, 1)
                    blocks(v, step)

                @block.tensor
                def _(pe):
                    def tr(b, s):
                        w(pe, nm_in, b, 0)
                        w(pe, nm_ev, b, 2)
                        for k in range(kt):
                            ins = pe.transpose(psM[s][:, k, 0:P], xs[s][:, k * P:(k + 1) * P], ident[:, :])
                        ins.then_inc(nm_tr, 1)

                    def mm(b, s):
                        w(pe, nm_ev, b, 0)
                        w(pe, nm_out, b, 2)
                        for k in range(kt):
                            ins = pe.matmul(psS[s][:, 0:cols], xT[s][:, k, :], W[:, k, 0:cols],
                                            start=(k == 0), stop=(k == kt - 1))
                        ins.then_inc(nm_mm, 1)

                    def step(b, s):
                        tr(b, s)
                        mm(b, s)
                    blocks(pe, step)

                @block.scalar
                def _(a):
                    def step(b, s):
                        w(a, nm_tr, b, 0)
                        w(a, nm_mm, b, 2)
                        a.activation(xT[s][:, 0:kt, :], psM[s][:, 0:kt, 0:P], ACT.Copy).then_inc(nm_ev, 1)
                        w(a, nm_mm, b, 0)
                        a.sem_inc(go, 1)
                        a.activation(dst[:, ds(b, 1), 0:cols].rearrange("p a c -> p (a c)"), psS[s][:, 0:cols],
                                     ACT.Copy).then_inc(nm_out, 1)
                    blocks(a, step)
        s_half = sem("s_half")
        halves = [0]

        def vector_act_vector(before, act_step, after):
            halves[0] += 2
            mark = halves[0]
            with nc.Block() as block:
                @block.vector
                def _(v):
                    before(v)
                    v.nop().then_inc(s_half, 1)
                    if after:
                        v.wait_ge(s_half, mark)
                        after(v)

                @block.scalar
                def _(a):
                    a.wait_ge(s_half, mark - 1)
                    act_step(a).then_inc(s_half, 1)

        o_ready, p1_done, a1_done, p2_done, gm_done, t_done, t2_done, mn_done, d_done, m_done = (
            sem(n) for n in ("onehot_ready", "transposed", "evacuated", "masked_ready", "tile_max_ready", "max_plus_dst",
                             "leaky_max_ready", "new_max_ready", "max_step_ready", "max_stored"))
        p3_done, z1_done, z2_done, z3_done, ex_done, hx_done, sg_done, sc_done, as_done, ac_done = (
            sem(n) for n in ("dst_terms_ready", "logit_sum", "logit_leaky", "logit_shifted", "exp_ready", "weighted_ready",
                             "segsum_ready", "rescale_ready", "acc_rescaled", "acc_added"))
        gathered = [sem(f"gathered{i}") for i in range(UN)]
        idx_ready = sem("idx_ready")
        idx_used = sem("idx_used")
        go = sem("go")
        base = {"group": {}, "gathered": 0, "idx_used": 0, "idx_ready": 0}

        def counts(n_src):
            mine = {}
            landed = TG * n_src * 16
            GB = base["gathered"]
            marks = (mine, base["idx_used"], base["idx_ready"])

            def start(s, per):
                if s.name not in mine:
                    mine[s.name] = base["group"].get(s.name, 0)
                    base["group"][s.name] = mine[s.name] + NG * per
                return mine[s.name]

            def w(eng, s, g, back=0, per=1):
                B = start(s, per)
                if isinstance(g, int) and g < back:
                    return
                eng.wait_ge(s, g * per + (B + (1 - back) * per))

            def rows_in(eng, g, slot):
                if isinstance(g, int):
                    eng.wait_ge(gathered[slot], GB + (g // UN + 1) * landed)
                else:
                    eng.wait_ge(gathered[slot], g * (landed // UN) + (GB + landed - slot * (landed // UN)))
            base["gathered"] += NG // UN * landed
            base["idx_used"] += NT * n_src
            base["idx_ready"] += NG // UN * n_src
            return w, rows_in, start, marks

        def gathers(block, sources, consumed, start, marks):
            n_src = len(sources)
            B, PB, IB = start(consumed, 1), marks[1], marks[2]

            @block.gpsimd
            def _(g):
                def body(j, first):
                    for half in range(2):
                        jj = j * 2 + half
                        if not (first):
                            g.wait_ge(idx_used, jj * (UN * TG * n_src) + (PB + (1 - 2) * UN * TG * n_src))
                            g.sem_inc(go, 1)
                        for q, (table, indices, dst, width) in enumerate(sources):
                            ins = g.tensor_copy(idx[half][:, q, :], indices[:, ds(jj * (UN * TG), UN * TG)])
                            ins.then_inc(idx_ready, 1)
                        g.wait_ge(idx_ready, jj * n_src + (IB + n_src))
                        g.sem_inc(go, 1)
                        for r in range(UN):
                            if not (first and half == 0):
                                g.wait_ge(consumed, jj * UN + (B + r + 1 - UN))
                                g.sem_inc(go, 1)
                            for t in range(TG):
                                for q, (table, indices, dst, width) in enumerate(sources):
                                    g.indirect_dma_start(
                                        out=dst[r][:, t, 0:width], out_offset=None, in_=table,
                                        in_offset=bass.IndirectOffsetOnAxis(
                                            ap=idx[half][:, q, r * TG + t:r * TG + t + 1], axis=0),
                                        engine_sem=idx_used).then_inc(gathered[r], 16)
                body(0, True)
                with g.Fori(1, NG // UN // 2) as j:
                    body(j, False)

        def gat_edges(table, C, Hn):
            W1c = C + 1
            RW = Hn * W1c
            RT = RW + (3 * Hn + 1) // 2
            w, rows_in, start, marks = counts(1)
            sel = head_sel if Hn == 4 else head_sel1
            H4 = [h[:, :, 0:RW].rearrange("p t (h c) -> p t h c", h=Hn) for h in H]
            Hx4 = [h[:, :, 0:RW].rearrange("p t (h c) -> p t h c", h=Hn) for h in Hx]
            AS = [[h[:, t, RW:RT].bitcast(bf16)[:, 0:3 * Hn] for t in range(TG)] for h in H]
            acc4 = lambda b: acc[:, ds(b, 1), 0:RW].rearrange("p a (h c) -> p (a h) c", h=Hn)
            Vb = lambda b: V[:, ds(b, 1), :].rearrange("p a c -> p (a c)")
            G = [psG[:, 16 * i:16 * i + 16].rearrange("p (t c) -> p t c", t=TG) for i in range(2)]

            with nc.Block() as block:
                gathers(block, [(table[:, :], e_src, H, RT)], hx_done, start, marks)

                @block.vector
                def _(v):
                    def onehot(g, s):
                        w(v, sg_done, g, UN)
                        w(v, p1_done, g, UN)
                        w(v, a1_done, g, UN, 3)
                        v.tensor_tensor(O[s][:, :, :], bc(iota_row[:, :], 1, TG),
                                        bc(e_ld[:, ds(g * TG, TG)], 2, P), ALU.is_equal).then_inc(o_ready, 1)

                    def logits(g, s):
                        i = s % 2
                        w(v, p3_done, g)
                        w(v, ex_done, g, UN)
                        v.tensor_tensor(z[s][:, :, 0:Hn], G[i][:, :, 0:Hn], H4[s][:, :, :, C], ALU.add).then_inc(z1_done, 1)
                        w(v, z1_done, g)
                        v.scalar_tensor_tensor(z[s][:, :, 0:Hn], z[s][:, :, 0:Hn], SLOPE, z[s][:, :, 0:Hn],
                                               ALU.mult, ALU.max).then_inc(z2_done, 1)
                        w(v, z2_done, g)
                        v.tensor_tensor(z[s][:, :, 0:Hn], z[s][:, :, 0:Hn], G[i][:, :, 4:4 + Hn],
                                        ALU.subtract).then_inc(z3_done, 1)

                    def maximum(g, s):
                        i = s % 2
                        b = v.value_load(blk[0:1, ds(g, 1)], min_val=0, max_val=NB - 1)
                        w(v, p2_done, g)
                        v.tensor_reduce(gm[:, 0:Hn], psM[i][:, :, 0:Hn * P].rearrange("p t (h e) -> p h t e", h=Hn),
                                        AX.XY, ALU.max).then_inc(gm_done, 1)
                        w(v, gm_done, g)
                        w(v, m_done, g, 1)
                        v.tensor_tensor(tm[:, 0:Hn], gm[:, 0:Hn], Vb(b)[:, 0:Hn], ALU.add).then_inc(t_done, 1)
                        w(v, t_done, g)
                        v.scalar_tensor_tensor(tm[:, 0:Hn], tm[:, 0:Hn], SLOPE, tm[:, 0:Hn], ALU.mult, ALU.max).then_inc(t2_done, 1)
                        w(v, t2_done, g)
                        v.tensor_tensor(mn[:, 0:Hn], tm[:, 0:Hn], Vb(b)[:, 4:4 + Hn], ALU.max).then_inc(mn_done, 1)
                        w(v, mn_done, g)
                        w(v, sc_done, g, UN)
                        v.tensor_tensor(dm[s][:, 0:Hn], Vb(b)[:, 4:4 + Hn], mn[:, 0:Hn], ALU.subtract).then_inc(d_done, 1)
                        w(v, d_done, g)
                        w(v, p3_done, g, 1)
                        v.tensor_tensor(Vb(b)[:, 4:4 + Hn], mn[:, 0:Hn], mn[:, 0:Hn], ALU.max).then_inc(m_done, 1)

                    def weigh(g, s):
                        i = s % 2
                        w(v, ex_done, g)
                        v.tensor_tensor(Hx4[i][:, :, :, 0:C], H4[s][:, :, :, 0:C],
                                        Hx4[i][:, :, :, C:C + 1].to_broadcast([P, TG, Hn, C]),
                                        ALU.mult).then_inc(hx_done, 1)

                    def accumulate(g, s):
                        i = s % 2
                        b = v.value_load(blk[0:1, ds(g, 1)], min_val=0, max_val=NB - 1)
                        w(v, sc_done, g)
                        w(v, ac_done, g, 1)
                        v.tensor_tensor(acc4(b), acc4(b), bc(sc[s][:, 0:Hn], 2, W1c), ALU.mult).then_inc(as_done, 1)
                        w(v, as_done, g)
                        w(v, sg_done, g)
                        v.tensor_tensor(acc4(b), acc4(b), psS[i][:, 0:RW].rearrange("p (h c) -> p h c", h=Hn),
                                        ALU.add).then_inc(ac_done, 1)

                    def step(g, s):
                        st = isinstance(g, int)
                        if not st or g + 1 < NG:
                            onehot(g + 1, (s + 1) % UN)
                        if not st or 1 <= g <= NG:
                            logits(g - 1, (s - 1) % UN)
                        if not st or g < NG:
                            maximum(g, s)
                        if not st or 1 <= g <= NG:
                            weigh(g - 1, (s - 1) % UN)
                        if not st or g >= 2:
                            accumulate(g - 2, (s - 2) % UN)
                    onehot(0, 0)
                    pipeline(v, step, NG + 2)

                @block.tensor
                def _(pe):
                    def transposes(g, s):
                        w(pe, o_ready, g)
                        rows_in(pe, g, s)
                        w(pe, a1_done, g, 1, 3)
                        for t in range(TG):
                            pe.transpose(psT[:, t * P:(t + 1) * P], O[s][:, t, :], ident[:, :])
                        for t in range(TG):
                            ins = pe.matmul(psT[0:3 * Hn, (TG + t) * P:(TG + t + 1) * P], AS[s][t], identb[:, :],
                                            start=True, stop=True)
                        ins.then_inc(p1_done, 1)

                    def masked(g, s):
                        i = s % 2
                        w(pe, a1_done, g, 0, 3)
                        w(pe, gm_done, g, 2)
                        for t in range(TG):
                            pe.matmul(psM[i][:, t, 0:Hn * P].rearrange("p (h e) -> p h e", h=Hn), NE[s][:, t, :],
                                      bc(neg_ident[:, :], 1, Hn), start=True, stop=False)
                            for h in range(Hn):
                                ins = pe.matmul(psM[i][:, t, h * P:(h + 1) * P], sel[:, h, :], asT[i][0:3 * Hn, t, :],
                                                start=False, stop=(h == Hn - 1))
                        ins.then_inc(p2_done, 1)

                    def dst_terms(g, s):
                        i = s % 2
                        b = pe.value_load(blk[0:1, ds(g, 1)], min_val=0, max_val=NB - 1)
                        w(pe, m_done, g)
                        w(pe, z3_done, g, 2)
                        for t in range(TG):
                            ins = pe.matmul(G[i][:, t, :], OT[s][:, t, :], Vb(b), start=True, stop=True)
                        ins.then_inc(p3_done, 1)

                    def segment_sum(g, s):
                        i = s % 2
                        w(pe, hx_done, g)
                        w(pe, ac_done, g, 2)
                        for t in range(TG):
                            ins = pe.matmul(psS[i][:, 0:RW], O[s][:, t, :], Hx[i][:, t, 0:RW], start=(t == 0), stop=(t == TG - 1))
                        ins.then_inc(sg_done, 1)

                    def step(g, s):
                        st = isinstance(g, int)
                        if not st or g + 1 < NG:
                            transposes(g + 1, (s + 1) % UN)
                        if not st or g < NG:
                            dst_terms(g, s)
                        if not st or g + 1 < NG:
                            masked(g + 1, (s + 1) % UN)
                        if not st or 1 <= g <= NG:
                            segment_sum(g - 1, (s - 1) % UN)
                    transposes(0, 0)
                    masked(0, 0)
                    pipeline(pe, step, NG + 1)

                @block.scalar
                def _(a):
                    def evacuate(g, s):
                        i = s % 2
                        w(a, o_ready, g)
                        w(a, p2_done, g, UN)
                        a.activation(NE[s][:, :, :], O[s][:, :, :], ACT.Identity, scale=-1.0, bias=ones[:, 0:1]).then_inc(a1_done, 1)
                        w(a, p1_done, g)
                        w(a, p2_done, g, 2)
                        a.activation(asT[i][0:3 * Hn, :, :], psT[0:3 * Hn, TG * P:2 * TG * P].rearrange("p (t e) -> p t e", t=TG),
                                     ACT.Copy).then_inc(a1_done, 1)
                        w(a, p3_done, g, UN)
                        a.activation(OT[s][:, :, :], psT[:, 0:TG * P].rearrange("p (t e) -> p t e", t=TG),
                                     ACT.Copy).then_inc(a1_done, 1)

                    def exps(g, s):
                        i = s % 2
                        w(a, z3_done, g)
                        w(a, sg_done, g, 2)
                        a.activation(Hx4[i][:, :, :, C], z[s][:, :, 0:Hn], ACT.Exp).then_inc(ex_done, 1)

                    def rescale(g, s):
                        i = s % 2
                        w(a, d_done, g)
                        w(a, ac_done, g, UN)
                        a.activation(sc[s][:, 0:Hn], dm[s][:, 0:Hn], ACT.Exp).then_inc(sc_done, 1)

                    def step(g, s):
                        st = isinstance(g, int)
                        if not st or g + 1 < NG:
                            evacuate(g + 1, (s + 1) % UN)
                        if not st or 1 <= g <= NG:
                            exps(g - 1, (s - 1) % UN)
                        if not st or g < NG:
                            rescale(g, s)
                    evacuate(0, 0)
                    pipeline(a, step, NG + 1)

        pj_done, gl_done, at1, at2, at_done = (sem(n) for n in (
            "projected", "gelu_ready", "dot_ready", "dot_bias_ready", "attn_ready"))

        def edge_attention(table, ev):
            w, rows_in, start, marks = counts(2)
            pE = [m[:, 0, 0:TG * D].rearrange("p (t c) -> p t c", t=TG) for m in psM]
            pA = [m[:, 0, TG * D:2 * TG * D].rearrange("p (t c) -> p t c", t=TG) for m in psM]
            pQ = [m[:, 1, 0:TG * (D + 1)].rearrange("p (t c) -> p t c", t=TG) for m in psM]
            G = [psG[:, 16 * i:16 * i + TG] for i in range(2)]
            V0 = lambda b: V[:, ds(b, 1), 0:1].rearrange("p a c -> p (a c)")
            accb = lambda b: acc[:, ds(b, 1), 0:D + 1].rearrange("p a c -> p (a c)")
            with nc.Block() as block:
                gathers(block, [(table[:, :], e_src, H, D), (ev, e_id, EV, D)], pj_done, start, marks)

                @block.vector
                def _(v):
                    def onehot(g, s):
                        w(v, sg_done, g, UN)
                        w(v, p1_done, g, UN)
                        w(v, a1_done, g, UN, 3)
                        v.tensor_tensor(O[s][:, :, :], bc(iota_row[:, :], 1, TG),
                                        bc(e_ld[:, ds(g * TG, TG)], 2, P), ALU.is_equal).then_inc(o_ready, 1)

                    def dots(g, s):
                        i = s % 2
                        w(v, gl_done, g)
                        w(v, p2_done, g, UN)
                        w(v, z3_done, g, UN)
                        for t in range(TG):
                            ins = v.tensor_tensor_reduce(junk[:, t, :], Tt[s][:, t, :], pQ[i][:, t, 0:D], 1.0, 0.0, ALU.mult,
                                                         ALU.add, accum_out=attn[s][:, t:t + 1])
                            ins.then_inc(at1, 1)
                            w(v, at1, g, 0, TG) if t == TG - 1 else None
                        v.tensor_tensor(attn[s][:, :], attn[s][:, :], pQ[i][:, :, D], ALU.add).then_inc(at2, 1)
                        w(v, at2, g)
                        v.tensor_tensor(attn[s][:, :], attn[s][:, :], e_w[:, ds(g * TG, TG)], ALU.mult).then_inc(at_done, 1)

                    def maximum(g, s):
                        i = s % 2
                        b = v.value_load(blk[0:1, ds(g, 1)], min_val=0, max_val=NB - 1)
                        w(v, p2_done, g)
                        v.tensor_reduce(gm[:, 0:1], pA[i], AX.XY, ALU.max).then_inc(gm_done, 1)
                        w(v, gm_done, g)
                        w(v, m_done, g, 1)
                        v.tensor_tensor(mn[:, 0:1], gm[:, 0:1], V0(b), ALU.max).then_inc(mn_done, 1)
                        w(v, mn_done, g)
                        w(v, sc_done, g, UN)
                        v.tensor_tensor(dm[s][:, 0:1], V0(b), mn[:, 0:1], ALU.subtract).then_inc(d_done, 1)
                        w(v, d_done, g)
                        w(v, p3_done, g, 1)
                        v.tensor_tensor(V0(b), mn[:, 0:1], mn[:, 0:1], ALU.max).then_inc(m_done, 1)

                    def logits(g, s):
                        i = s % 2
                        w(v, p3_done, g)
                        w(v, ex_done, g, UN)
                        v.tensor_tensor(z[s][:, :, 0], attn[s][:, :], G[i], ALU.subtract).then_inc(z3_done, 1)

                    def weigh(g, s):
                        i = s % 2
                        w(v, ex_done, g)
                        v.tensor_tensor(Hx[i][:, :, 0:D], Tt[s][:, :, :], Hx[i][:, :, D:D + 1].to_broadcast([P, TG, D]),
                                        ALU.mult).then_inc(hx_done, 1)

                    def accumulate(g, s):
                        i = s % 2
                        b = v.value_load(blk[0:1, ds(g, 1)], min_val=0, max_val=NB - 1)
                        w(v, sc_done, g)
                        w(v, ac_done, g, 1)
                        w(v, sg_done, g)
                        v.scalar_tensor_tensor(accb(b), accb(b), sc[s][:, 0:1], psS[i][:, 0:D + 1], ALU.mult,
                                               ALU.add).then_inc(ac_done, 1)

                    def step(g, s):
                        st = isinstance(g, int)
                        if not st or g + 1 < NG:
                            onehot(g + 1, (s + 1) % UN)
                        if not st or 2 <= g <= NG + 1:
                            logits(g - 2, (s - 2) % UN)
                        if not st or 1 <= g <= NG:
                            maximum(g - 1, (s - 1) % UN)
                        if not st or g < NG:
                            dots(g, s)
                        if not st or 2 <= g <= NG + 1:
                            weigh(g - 2, (s - 2) % UN)
                        if not st or 3 <= g:
                            accumulate(g - 3, (s - 3) % UN)
                    onehot(0, 0)
                    pipeline(v, step, NG + 3)

                @block.tensor
                def _(pe):
                    def transposes(g, s):
                        w(pe, o_ready, g)
                        rows_in(pe, g, s)
                        w(pe, a1_done, g, 1, 3)
                        for t in range(TG):
                            pe.transpose(psT[:, t * P:(t + 1) * P], O[s][:, t, :], ident[:, :])
                        for t in range(TG):
                            ins = pe.transpose(psT[:, (TG + t) * P:(TG + t + 1) * P], EV[s][:, t, :], ident[:, :])
                        ins.then_inc(p1_done, 1)

                    def project(g, s):
                        i = s % 2
                        b = pe.value_load(blk[0:1, ds(g, 1)], min_val=0, max_val=NB - 1)
                        w(pe, a1_done, g, 0, 3)
                        w(pe, gl_done, g, 2)
                        w(pe, at2, g, 2)
                        for t in range(TG):
                            pe.matmul(pE[i][:, t, :], evT[i][:, t, :], WT2[:, :], start=True, stop=False)
                            pe.matmul(pE[i][:, t, :], ident[:, :], H[s][:, t, 0:D], start=False, stop=True)
                            ins = pe.matmul(pQ[i][:, t, :], OT[s][:, t, :], QK[:, ds(b, 1), :].rearrange("p a c -> p (a c)"),
                                            start=True, stop=True)
                        ins.then_inc(pj_done, 1)

                    def masked(g, s):
                        i = s % 2
                        w(pe, at_done, g)
                        w(pe, gm_done, g, 2)
                        for t in range(TG):
                            pe.matmul(pA[i][:, t, :], NE[s][:, t, :], neg_ident[:, :], start=True, stop=False)
                            ins = pe.matmul(pA[i][:, t, :], attn[s][:, t:t + 1].to_broadcast([P, P]), ident[:, :],
                                            start=False, stop=True)
                        ins.then_inc(p2_done, 1)

                    def dst_max(g, s):
                        i = s % 2
                        b = pe.value_load(blk[0:1, ds(g, 1)], min_val=0, max_val=NB - 1)
                        w(pe, m_done, g)
                        w(pe, z3_done, g, 2)
                        for t in range(TG):
                            ins = pe.matmul(G[i][:, t:t + 1], OT[s][:, t, :], V0(b), start=True, stop=True)
                        ins.then_inc(p3_done, 1)

                    def segment_sum(g, s):
                        i = s % 2
                        w(pe, hx_done, g)
                        w(pe, ac_done, g, 2)
                        for t in range(TG):
                            ins = pe.matmul(psS[i][:, 0:D + 1], O[s][:, t, :], Hx[i][:, t, 0:D + 1], start=(t == 0),
                                            stop=(t == TG - 1))
                        ins.then_inc(sg_done, 1)

                    def step(g, s):
                        st = isinstance(g, int)
                        if not st or g + 1 < NG:
                            transposes(g + 1, (s + 1) % UN)
                        if not st or 1 <= g <= NG:
                            dst_max(g - 1, (s - 1) % UN)
                        if not st or g + 1 < NG:
                            project(g + 1, (s + 1) % UN)
                        if not st or g < NG:
                            masked(g, s)
                        if not st or 2 <= g <= NG + 1:
                            segment_sum(g - 2, (s - 2) % UN)
                    transposes(0, 0)
                    project(0, 0)
                    pipeline(pe, step, NG + 2)

                @block.scalar
                def _(a):
                    def evacuate(g, s):
                        i = s % 2
                        w(a, o_ready, g)
                        w(a, p2_done, g, UN)
                        a.activation(NE[s][:, :, :], O[s][:, :, :], ACT.Identity, scale=-1.0, bias=ones[:, 0:1]).then_inc(a1_done, 1)
                        w(a, p1_done, g)
                        w(a, pj_done, g, 2)
                        w(a, p3_done, g, UN)
                        a.activation(evT[i][:, :, :], psT[:, TG * P:2 * TG * P].rearrange("p (t e) -> p t e", t=TG),
                                     ACT.Copy).then_inc(a1_done, 1)
                        a.activation(OT[s][:, :, :], psT[:, 0:TG * P].rearrange("p (t e) -> p t e", t=TG),
                                     ACT.Copy).then_inc(a1_done, 1)

                    def gelu(g, s):
                        i = s % 2
                        w(a, pj_done, g)
                        w(a, hx_done, g, UN)
                        w(a, at1, g, UN, TG)
                        a.activation(Tt[s][:, :, :], pE[i], ACT.Gelu).then_inc(gl_done, 1)

                    def exps(g, s):
                        i = s % 2
                        w(a, z3_done, g)
                        w(a, sg_done, g, 2)
                        a.activation(Hx[i][:, :, D], z[s][:, :, 0], ACT.Exp).then_inc(ex_done, 1)

                    def rescale(g, s):
                        w(a, d_done, g)
                        w(a, ac_done, g, UN)
                        a.activation(sc[s][:, 0:1], dm[s][:, 0:1], ACT.Exp).then_inc(sc_done, 1)

                    def step(g, s):
                        st = isinstance(g, int)
                        if not st or g + 1 < NG:
                            evacuate(g + 1, (s + 1) % UN)
                        if not st or 2 <= g <= NG + 1:
                            exps(g - 2, (s - 2) % UN)
                        if not st or 1 <= g <= NG:
                            rescale(g - 1, (s - 1) % UN)
                        if not st or g + 1 < NG:
                            gelu(g + 1, (s + 1) % UN)
                    evacuate(0, 0)
                    gelu(0, 0)
                    pipeline(a, step, NG + 2)

        def edge_sums(table):
            w, rows_in, start, marks = counts(1)
            accb = lambda b: acc[:, ds(b, 1), 0:D].rearrange("p a c -> p (a c)")
            with nc.Block() as block:
                gathers(block, [(table[:, :], e_src, H, D)], sg_done, start, marks)

                @block.vector
                def _(v):
                    def onehot(g, s):
                        w(v, sg_done, g, UN)
                        v.tensor_tensor(O[s][:, :, :], bc(iota_row[:, :], 1, TG),
                                        bc(e_ld[:, ds(g * TG, TG)], 2, P), ALU.is_equal).then_inc(o_ready, 1)

                    def accumulate(g, s):
                        i = s % 2
                        b = v.value_load(blk[0:1, ds(g, 1)], min_val=0, max_val=NB - 1)
                        w(v, ac_done, g, 1)
                        w(v, sg_done, g)
                        v.tensor_tensor(accb(b), accb(b), psS[i][:, 0:D], ALU.add).then_inc(ac_done, 1)

                    def step(g, s):
                        st = isinstance(g, int)
                        if not st or g + 1 < NG:
                            onehot(g + 1, (s + 1) % UN)
                        if not st or g >= 1:
                            accumulate(g - 1, (s - 1) % UN)
                    onehot(0, 0)
                    pipeline(v, step, NG + 1)

                @block.tensor
                def _(pe):
                    def step(g, s):
                        i = s % 2
                        w(pe, o_ready, g)
                        rows_in(pe, g, s)
                        w(pe, ac_done, g, 2)
                        for t in range(TG):
                            ins = pe.matmul(psS[i][:, 0:D], O[s][:, t, :], H[s][:, t, 0:D], start=(t == 0), stop=(t == TG - 1))
                        ins.then_inc(sg_done, 1)
                    pipeline(pe, step, NG)

        def loads_of(pairs):
            with nc.Block() as block:
                @block.sync
                def _(sp):
                    for dst, src in pairs:
                        load(sp, dst, src)
                    loaded(sp)

        def vector_part(program):
            with nc.Block() as block:
                @block.vector
                def _(v):
                    program(v)

        def store_table(table, cols):
            with nc.Block() as block:
                @block.sync
                def _(sp):
                    load(sp, table.rearrange("(b p) c -> p b c", p=P), Z[:, :, 0:cols])
                    loaded(sp)

        def head_rows(ap, C, Hn):
            return ap[:, :, 0:Hn * (C + 1)].rearrange("p b (h c) -> p b h c", h=Hn)

        def denominators(v, den, Hn):
            r = small[:, 0, 0:NB * Hn].rearrange("p (b h) -> p b h", h=Hn)
            link(v, v.tensor_scalar(r, den, EPS_SM, None, ALU.add))
            link(v, v.reciprocal(r, r))
            return r

        def row(i, cols):
            return bc(brow[:, i, 0:cols], 1, NB)

        def layernorm_into(src, dst, tmp, gamma=None, beta=None):
            mean, var = small[:, 1, 0:NB], small[:, 2, 0:NB]

            def before(v):
                link(v, v.reduce_sum(mean, src, AX.X))
                link(v, v.tensor_scalar(mean, mean, 1.0 / D, None, ALU.mult))
                link(v, v.tensor_tensor(src, src, bc(mean, 2, D), ALU.subtract))
                link(v, v.tensor_tensor(tmp, src, src, ALU.mult))
                link(v, v.reduce_sum(var, tmp, AX.X))
                link(v, v.tensor_scalar(var, var, 1.0 / D, EPS_LN, ALU.mult, ALU.add))

            def after(v):
                link(v, v.reciprocal(var, var))
                link(v, v.tensor_tensor(dst, src, bc(var, 2, D), ALU.mult))
                if gamma is not None:
                    link(v, v.tensor_tensor(dst, dst, gamma, ALU.mult))
                    link(v, v.tensor_tensor(dst, dst, beta, ALU.add))
            vector_act_vector(before, lambda a: a.activation(var, var, ACT.Sqrt), after)

        def gat_layer(name, src, K, W, a_s, a_d, b, C, Hn, own_edge=False):
            kt = K // P
            HC, RW = Hn * C, Hn * (C + 1)
            RT = RW + (3 * Hn + 1) // 2
            table = nc.dram_tensor(f"table_{name}", [NB * P, RT], f32).ap()
            loads_of([(WR[:, 0:kt, 0:HC], W.rearrange("(k p) n -> p k n", p=P)),
                      (vec[:, 0, 0:HC], rows(a_s.rearrange("h c -> (h c)"))),
                      (vec[:, 1, 0:HC], rows(a_d.rearrange("h c -> (h c)"))),
                      (brow[:, 0, 0:HC], rows(b))])

            def weights(v):
                hc = lambda ap: ap.rearrange("p (h c) -> p h c", h=Hn)
                for k in range(kt):
                    own = WA[:, k, 0:RW].rearrange("p (h c) -> p h c", h=Hn)
                    link(v, v.tensor_copy(own[:, :, 0:C], hc(WR[:, k, 0:HC])))
                    link(v, v.tensor_tensor(wtmp[:, 0:HC], WR[:, k, 0:HC], vec[:, 0, 0:HC], ALU.mult))
                    link(v, v.reduce_sum(own[:, :, C], hc(wtmp[:, 0:HC]), AX.X))
                    link(v, v.tensor_tensor(wtmp[:, 0:HC], WR[:, k, 0:HC], vec[:, 1, 0:HC], ALU.mult))
                    link(v, v.reduce_sum(WA[:, k, RW:RW + Hn], hc(wtmp[:, 0:HC]), AX.X))
            vector_part(weights)
            node_matmul(src, K, WA, RW + Hn, Z)

            def tables(v):
                link(v, v.memset(V[:, :, :], NEG))
                link(v, v.tensor_copy(V[:, :, 0:Hn], Z[:, :, RW:RW + Hn]))
                a_src = head_rows(Z, C, Hn)[:, :, :, C]
                if own_edge:
                    top = V[:, :, 4:4 + Hn]
                    link(v, v.tensor_tensor(top, a_src, V[:, :, 0:Hn], ALU.add))
                    link(v, v.scalar_tensor_tensor(top, top, SLOPE, top, ALU.mult, ALU.max))
                    link(v, v.tensor_copy(acc[:, :, 0:RW], Z[:, :, 0:RW]))
                    link(v, v.memset(head_rows(acc, C, Hn)[:, :, :, C], 1.0))
                else:
                    link(v, v.memset(acc[:, :, 0:RW], 0.0))
                link(v, v.memset(Z[:, :, RW:RT], 0.0))
                parts = Z[:, :, RW:RT].bitcast(bf16)
                rest = small[:, 3, 0:NB * Hn].rearrange("p (b h) -> p b h", h=Hn)
                pt = lambda q: parts[:, :, q:q + 3 * (Hn - 1) + 1:3] if Hn > 1 else parts[:, :, q:q + 1]
                link(v, v.tensor_copy(pt(0), a_src))
                link(v, v.tensor_tensor(rest, a_src, pt(0), ALU.subtract))
                link(v, v.tensor_copy(pt(1), rest))
                link(v, v.tensor_tensor(rest, rest, pt(1), ALU.subtract))
                link(v, v.tensor_copy(pt(2), rest))
            vector_part(tables)
            store_table(table, RT)
            gat_edges(table, C, Hn)

        def heads_out(v, dst, C, Hn):
            a4 = head_rows(acc, C, Hn)
            r = denominators(v, a4[:, :, :, C], Hn)
            link(v, v.tensor_tensor(dst.rearrange("p b (h c) -> p b h c", h=Hn), a4[:, :, :, 0:C], bc(r, 3, C), ALU.mult))
            link(v, v.tensor_tensor(dst, dst, row(0, Hn * C), ALU.add))

        def elu_out():
            def before(v):
                heads_out(v, Y[:, :, :], 64, 4)
                link(v, v.tensor_scalar(Z[:, :, 0:256], Y[:, :, :], 0.0, None, ALU.min))

            def after(v):
                link(v, v.scalar_tensor_tensor(Y[:, :, :], Y[:, :, :], 0.0, Z[:, :, 0:256], ALU.max, ALU.add))
                link(v, v.tensor_scalar(Y[:, :, :], Y[:, :, :], 1.0, None, ALU.subtract))
            vector_act_vector(before, lambda a: a.activation(Z[:, :, 0:256], Z[:, :, 0:256], ACT.Exp), after)

        def add_norm(src):
            vector_part(lambda v: link(v, v.tensor_tensor(X[:, :, :], X[:, :, :], src, ALU.add)))
            layernorm_into(X[:, :, :], X[:, :, :], Z[:, :, 0:D])

        def transposed_weight(dst):
            halves[0] += 1
            mark = halves[0]
            with nc.Block() as block:
                @block.tensor
                def _(pe):
                    pe.transpose(psS[0][:, 0:P], WR[:, 0, 0:D], ident[:, :]).then_inc(s_half, 1)

                @block.vector
                def _(v):
                    v.wait_ge(s_half, mark)
                    link(v, v.tensor_copy(dst, psS[0][:, 0:P]))

        Yl, Yr = Y[:, :, 0:D], Y[:, :, D:2 * D]

        def finish(src):
            with nc.Block() as block:
                @block.sync
                def _(sp):
                    load(sp, out[0:(NB - 1) * P, :].rearrange("(b p) c -> p b c", p=P), src[:, 0:NB - 1, :])
                    load(sp, out[(NB - 1) * P:N, :], src[0:LASTN, NB - 1, :])
                    loaded(sp)

        def read_x():
            x = T["x"]
            vector_part(lambda v: link(v, v.memset(X[:, NB - 1, :], 0.0)))
            loads_of([(X[:, 0:NB - 1, :], x[0:(NB - 1) * P, :].rearrange("(b p) c -> p b c", p=P)),
                      (X[0:LASTN, NB - 1, :], x[(NB - 1) * P:N, :])])

        setup()
        read_x()
        gat_layer("l0a", X[:, :, :], D, T["L0_gnn_W0"], T["L0_gnn_as0"], T["L0_gnn_ad0"], T["L0_gnn_b0"], 64, 4, own_edge=True)
        elu_out()
        if stop == "l0a":
            return finish(Yl)
        gat_layer("l0b", Y[:, :, :], 256, T["L0_gnn_W1"], T["L0_gnn_as1"], T["L0_gnn_ad1"], T["L0_gnn_b1"], 64, 4, own_edge=True)
        elu_out()
        gat_layer("l0c", Y[:, :, :], 256, T["L0_gnn_W2"], T["L0_gnn_as2"], T["L0_gnn_ad2"], T["L0_gnn_b2"], 128, 1, own_edge=True)
        vector_part(lambda v: heads_out(v, Yl, 128, 1))
        add_norm(Yl)
        if stop == "l0":
            return finish(X)

        gat_layer("l1a", X[:, :, :], D, T["L1_gnn_W0"], T["L1_gnn_att_src0"], T["L1_gnn_att_dst0"], T["L1_gnn_b0"], 32, 4)

        def relu_out(v):
            heads_out(v, Yl, 32, 4)
            link(v, v.tensor_scalar(Yl, Yl, 0.0, None, ALU.max))
        vector_part(relu_out)
        gat_layer("l1b", Yl, D, T["L1_gnn_W1"], T["L1_gnn_att_src1"], T["L1_gnn_att_dst1"], T["L1_gnn_b1"], 32, 4)
        vector_part(lambda v: heads_out(v, Yl, 32, 4))
        add_norm(Yl)
        if stop == "l1":
            return finish(X)

        Wt = T["L2_gnn_Wt"]
        loads_of([(brow[:, 0, 0:D], rows(T["L2_gnn_gamma"])), (brow[:, 1, 0:D], rows(T["L2_gnn_beta"])),
                  (brow[:, 2, 0:D], rows(T["L2_gnn_bt"])), (brow[:, 3, 0:D], rows(T["L2_gnn_bq"])),
                  (WA[:, 0, 0:D], Wt[0:D, :]), (WT2[:, :], Wt[D:2 * D, :])])
        vector_part(lambda v: link(v, v.tensor_copy(Yr, X[:, :, :])))
        layernorm_into(Yr, Yl, Z[:, :, 0:D], row(0, D), row(1, D))
        table2 = nc.dram_tensor("table_l2", [NB * P, D], f32).ap()
        node_matmul(Yl, D, WA, D, Z)
        vector_part(lambda v: link(v, v.tensor_tensor(Z[:, :, 0:D], Z[:, :, 0:D], row(2, D), ALU.add)))
        store_table(table2, D)
        loads_of([(WA[:, 0, 0:D], T["L2_gnn_Wq"]), (WR[:, 0, 0:D], T["L2_gnn_Wk"]),
                  (vec[:, 0, 0:1], T["L2_gnn_bk"].rearrange("(a b) -> a b", b=1))])
        node_matmul(Yl, D, WA, D, Yr)
        vector_part(lambda v: link(v, v.tensor_tensor(Yr, Yr, row(3, D), ALU.add)))
        transposed_weight(WA[:, 0, 0:D])
        vector_part(lambda v: link(v, v.tensor_copy(WA[:, 0, D:D + 1], vec[:, 0, 0:1])))
        node_matmul(Yr, D, WA, D + 1, QK)

        def clear2(v):
            link(v, v.memset(V[:, :, :], NEG))
            link(v, v.memset(acc[:, :, 0:D + 1], 0.0))
        vector_part(clear2)
        edge_attention(table2, T["edge_attr_128"])
        loads_of([(WA[:, 0, 0:D], T["L2_gnn_Wv"]), (brow[:, 0, 0:D], rows(T["L2_gnn_bv"]))])

        def averages(v):
            r = denominators(v, acc[:, :, D:D + 1], 1)
            link(v, v.tensor_tensor(Yl, acc[:, :, 0:D], r.to_broadcast([P, NB, D]), ALU.mult))
            link(v, v.tensor_tensor(small[:, 1, 0:NB].rearrange("p (b a) -> p b a", a=1), acc[:, :, D:D + 1], r, ALU.mult))
        vector_part(averages)
        node_matmul(Yl, D, WA, D, Z)

        def value_bias(v):
            link(v, v.tensor_tensor(Yl, bc(small[:, 1, 0:NB], 2, D), row(0, D), ALU.mult))
            link(v, v.tensor_tensor(Z[:, :, 0:D], Z[:, :, 0:D], Yl, ALU.add))
        vector_act_vector(value_bias, lambda a: a.activation(Yl, Z[:, :, 0:D], ACT.Gelu), None)
        vector_part(lambda v: link(v, v.tensor_tensor(Yl, Yl, X[:, :, :], ALU.add)))
        add_norm(Yl)
        if stop == "l2":
            return finish(X)

        loads_of([(WR[:, 0, 0:D], T["L3_gnn_W1"]), (brow[:, 0, 0:D], rows(T["L3_gnn_b1"])),
                  (brow[:, 1, 0:D], rows(T["L3_gnn_b2"]))])
        transposed_weight(WA[:, 0, 0:D])
        node_matmul(X[:, :, :], D, WA, D, Z)
        table3 = nc.dram_tensor("table_l3", [NB * P, D], f32).ap()

        def bias_relu(v, dst, i):
            link(v, v.tensor_tensor(dst, dst, row(i, D), ALU.add))
            link(v, v.tensor_scalar(dst, dst, 0.0, None, ALU.max))

        def messages(v):
            bias_relu(v, Z[:, :, 0:D], 0)
            link(v, v.memset(acc[:, :, 0:D], 0.0))
        vector_part(messages)
        store_table(table3, D)
        edge_sums(table3)
        loads_of([(WR[:, 0, 0:D], T["L3_gnn_W2"])])
        transposed_weight(WA[:, 0, 0:D])
        vector_part(lambda v: link(v, v.tensor_tensor(Yl, acc[:, :, 0:D], X[:, :, :], ALU.add)))
        node_matmul(Yl, D, WA, D, Yr)
        vector_part(lambda v: bias_relu(v, Yr, 1))
        add_norm(Yr)
        finish(X)


def kernel(**inputs):
    import numpy as _np
    import concourse.bacc as _bacc
    from concourse import mybir as _mybir
    from concourse.bass_utils import run_bass_kernel_spmd as _run

    nc = _bacc.Bacc("TRN2", target_bir_lowering=False, num_devices=1)
    arrays, T = {}, {}
    for name, a in inputs.items():
        a = _np.ascontiguousarray(a)
        arrays[f"in_{name}"] = a
        T[name] = nc.dram_tensor(f"in_{name}", a.shape, _mybir.dt.from_np(a.dtype), kind="ExternalInput").ap()
    out = nc.dram_tensor("out_0", (N, D), f32, kind="ExternalOutput").ap()
    gnn(nc, T, out)
    r = _run(nc, [arrays], core_ids=[0])
    return r.results[0]["out_0"]
```

```python
import concourse.bass as bass
from concourse import mybir
from contextlib import ExitStack

f32 = mybir.dt.float32
bf16 = mybir.dt.bfloat16
i32 = mybir.dt.int32
u32 = mybir.dt.uint32
ALU = mybir.AluOpType
ACT = mybir.ActivationFunctionType
AX = mybir.AxisListType
ds = bass.ds

N = 3125
E = 53125
P = 128
NB = -(-N // P)
LASTN = N - (NB - 1) * P
D = 128
TG = 2
GE = TG * P
NG = (E + NB * (GE - 1)) // GE
NT = NG * TG
EC = -(-E // P)
EFULL = E // EC
EREST = E - EFULL * EC
UN = 8
IG = 4
NEG = -1.0e30
SLOPE = 0.2
EPS_SM = 1e-16
EPS_LN = 1e-5
PEEL = UN
assert NG % UN == 0 and UN == 2 * IG


def bc(ap, axis, n):
    a = ap.unsqueeze(axis)
    shape = list(a.shape)
    shape[axis] = n
    return a.to_broadcast(shape)


def rows(ap1d):
    return ap1d.partition_broadcast(P)


def g_in(g, ahead):
    return not isinstance(g, int) or 0 <= g + ahead < NG


def pipeline(nc, blk, eng, step, last, lo=0, hi=0):
    def blocks(first, at, count):
        if not count:
            return None
        _, values = nc.values_load_multi_w_load_instructions(
            blk[0:1, ds(first, count)], engines=[eng.engine], min_val=0, max_val=NB - 1,
            skip_runtime_bounds_check_because="the setup clamps the blocks to 0 .. NB - 1")
        return {at + i: x for i, x in enumerate(values)}

    def steps(first, count, loaded, at):
        for r in range(count):
            step(first + r, (at + r) % UN, lambda a, r=r: loaded[r + a])
    front = blocks(0, 0, UN + hi)
    steps(0, PEEL, front, 0)
    with eng.Fori(0, (NG - 2 * PEEL) // UN) as j:
        mid = blocks(j * UN + (PEEL + lo), lo, UN + hi - lo)
        steps(j * UN + PEEL, UN, mid, 0)
    back = blocks(NG - PEEL + lo, lo, PEEL - lo)
    steps(NG - PEEL, last - (NG - PEEL), back, 0)


def gnn(nc, T, out, stop=None):
    ctx = ExitStack()
    sb = lambda n, s, d=f32: ctx.enter_context(nc.sbuf_tensor(n, s, d))
    sem = lambda n: ctx.enter_context(nc.semaphore(n))
    with ctx:
        ident = sb("ident", [P, P])
        identb = sb("identb", [P, P], bf16)
        neg_ident = sb("neg_ident", [P, P], bf16)
        iota_row = sb("iota_row", [P, P], bf16)
        ones = sb("ones", [P, P])
        tri = sb("tri", [P, P])
        head_sel = sb("head_sel", [12, 4, P], bf16)
        head_sel1 = sb("head_sel1", [3, 1, P], bf16)
        e_src = sb("e_src", [P, NT], u32)
        e_id = sb("e_id", [P, NT], u32)
        e_ld = sb("e_ld", [P, NT])
        e_w = sb("e_w", [P, NT])
        blk = sb("blk", [1, NG + UN], i32)
        X = sb("X", [P, NB, D])
        Y = sb("Y", [P, NB, 256])
        Z = sb("Z", [P, NB, 266])
        acc = sb("acc", [P, NB, 260])
        QK = sb("QK", [P, NB, D + 1])
        V = sb("V", [P, NB, 8])
        small = sb("small", [P, 4, NB * 4])
        WA = sb("WA", [P, 2, 264])
        WR = sb("WR", [P, 2, 256])
        WT2 = sb("WT2", [P, D])
        vec = sb("vec", [P, 2, 256])
        brow = sb("brow", [P, 4, 256])
        wtmp = sb("wtmp", [P, 256])
        H = [sb(f"H{i}", [P, TG, 266]) for i in range(UN)]
        EV = [sb(f"EV{i}", [P, TG, D]) for i in range(UN)]
        idx = [sb(f"idx{i}", [P, 2, IG * TG], u32) for i in range(2)]
        O = [sb(f"O{i}", [P, TG, P]) for i in range(UN)]
        NE = [sb(f"NE{i}", [P, TG, P], bf16) for i in range(UN)]
        OT = [sb(f"OT{i}", [P, TG, P]) for i in range(UN)]
        asT = [sb(f"asT{i}", [12, TG, P], bf16) for i in range(4)]
        evT = [sb(f"evT{i}", [P, TG, P]) for i in range(4)]
        Hx = [sb(f"Hx{i}", [P, TG, 260]) for i in range(4)]
        Tt = [sb(f"Tt{i}", [P, TG, D]) for i in range(UN)]
        attn = [sb(f"attn{i}", [P, TG]) for i in range(UN)]
        z = [sb(f"z{i}", [P, TG, 4]) for i in range(UN)]
        gm = sb("gm", [P, 4])
        tm = sb("tm", [P, 4])
        mn = sb("mn", [P, 4])
        dm = [sb(f"dm{i}", [P, 4]) for i in range(UN)]
        sc = [sb(f"sc{i}", [P, 4]) for i in range(UN)]
        junk = sb("junk", [P, TG, D])
        pb = lambda n, s: ctx.enter_context(nc.psum_tensor(n, s, f32))
        psM = [pb(f"psM{i}", [P, TG, 512]) for i in range(2)]
        psT = pb("psT", [P, 512])
        psTb = psT[:, 0:TG * P // 2].bitcast(bf16)
        psG = pb("psG", [P, 512])
        psS = [pb(f"psS{i}", [P, 512]) for i in range(2)]

        s_step = sem("s_step")
        s_load = sem("s_load")
        steps = [0]
        loads = [0]

        def link(eng, ins):
            steps[0] += 1
            ins.then_inc(s_step, 1)
            eng.wait_ge(s_step, steps[0])

        def load(eng, dst, src):
            loads[0] += 16
            eng.dma_start(dst, src).then_inc(s_load, 16)

        def loaded(eng):
            eng.wait_ge(s_load, loads[0])

        def setup():
            with ExitStack() as c2:
                sb2 = lambda n, s, d=f32: c2.enter_context(nc.sbuf_tensor(n, s, d))
                free = {"Y": [Y[:, :, :].rearrange("p b c -> p (b c)"), 0], "acc": [acc[:, :, :].rearrange("p b c -> p (b c)"), 0]}

                def carve(cols, dt=f32, where="Y"):
                    flat, at = free[where]
                    free[where][1] += cols
                    part = flat[:, at:at + cols]
                    return part if dt == f32 else part.bitcast(dt)
                dst_i, kb_i, ld_i, pos = (carve(EC, i32) for _ in range(4))
                src_i = carve(EC, i32)
                w_in, kb, eq, cnt, rank, one_c = (carve(EC) for _ in range(6))
                dest = carve(EC, u32)
                bid, tot, base = (carve(NB) for _ in range(3))
                ngr = carve(4 * NB).rearrange("p (k b) -> p k b", b=NB)
                ngi = carve(NB, i32)
                jio, jblk = carve(NG)[0:1, :], carve(NG)[0:1, :]
                jcmp = carve(NG * NB, where="acc")[0:1, :].rearrange("p (g b) -> p g b", g=NG)
                rec = X[:, :, :].rearrange("p b c -> p (b c)")[:, 0:EC * 4].rearrange("p (c f) -> p c f", f=4)
                pad = Z[:, :, :].rearrange("p b c -> p (b c)")[:, 0:NT * 4].rearrange("p (t f) -> p t f", f=4)
                SC = 8
                rslot = [sb2(f"rslot{i}", [P, SC, 4]) for i in range(2)]
                dslot = [sb2(f"dslot{i}", [P, SC], u32) for i in range(2)]
                sorted_e = nc.dram_tensor("sorted_e", [P * NT, 4], f32).ap()
                s_const = sem("s_const")
                s_in = sem("s_in")
                s_eq = sem("s_eq"); s_cnt = sem("s_cnt"); s_mul = sem("s_mul"); s_rank = sem("s_rank")
                s_tot = sem("s_tot"); s_pre = sem("s_pre"); s_rec = sem("s_rec")
                s_padded = sem("s_padded")
                s_slot = sem("s_slot"); s_scat = [sem("s_scat0"), sem("s_scat1")]
                s_back = sem("s_back")
                s_pool = sem("s_pool")

                with nc.Block() as block:
                    @block.gpsimd
                    def _(g):
                        n = [0]

                        def own(ins):
                            n[0] += 1
                            ins.then_inc(s_pool, 1)
                            g.wait_ge(s_pool, n[0])
                        own(g.memset(dst_i[:, :], 99 * P))
                        own(g.memset(src_i[:, :], 0))
                        own(g.memset(w_in[:, :], 0.0))
                        for t, name in ((dst_i, "dst"), (src_i, "src"), (w_in, "edge_weight1")):
                            flat = T[name].rearrange("a b -> (a b)") if name == "edge_weight1" else T[name]
                            g.dma_start(t[0:EFULL, :], flat[0:EFULL * EC].rearrange("(p c) -> p c", c=EC)).then_inc(s_in, 16)
                            g.dma_start(t[EFULL:EFULL + 1, 0:EREST],
                                        flat[EFULL * EC:E].rearrange("(p c) -> p c", c=EREST)).then_inc(s_in, 16)
                        own(g.memset(ones[:, :], 1.0))
                        own(g.memset(ident[:, :], 0.0))
                        own(g.memset(head_sel[:, :, :], 1.0))
                        own(g.memset(head_sel1[:, :, :], 1.0))
                        own(g.affine_select(out=ident[:, :], in_=ident[:, :], compare_op=ALU.not_equal, fill=1.0,
                                            base=0, pattern=[[-1, P]], channel_multiplier=1))
                        own(g.affine_select(out=tri[:, :], in_=ones[:, :], compare_op=ALU.is_gt, fill=0.0,
                                            base=0, pattern=[[1, P]], channel_multiplier=-1))
                        own(g.affine_select(out=head_sel[:, :, :], in_=head_sel[:, :, :], compare_op=ALU.is_ge, fill=0.0,
                                            base=0, pattern=[[-3, 4], [0, P]], channel_multiplier=1))
                        own(g.affine_select(out=head_sel[:, :, :], in_=head_sel[:, :, :], compare_op=ALU.is_ge, fill=0.0,
                                            base=2, pattern=[[3, 4], [0, P]], channel_multiplier=-1))
                        own(g.iota(kb_i[:, 0:P], pattern=[[1, P]], base=0, channel_multiplier=0))
                        own(g.tensor_copy(iota_row[:, :], kb_i[:, 0:P]))
                        own(g.tensor_copy(bid[:, :], kb_i[:, 0:NB]))
                        own(g.iota(kb_i[0:1, 0:NG], pattern=[[1, NG]], base=0, channel_multiplier=0))
                        own(g.tensor_copy(jio[:, :], kb_i[0:1, 0:NG]))
                        own(g.iota(ld_i[:, :], pattern=[[1, EC]], base=0, channel_multiplier=EC))
                        own(g.tensor_copy(rec[:, :, 2], ld_i[:, :]))
                        own(g.memset(one_c[:, :], 1.0))
                        own(g.memset(pad[:, :, :], 0.0))
                        own(g.memset(pad[:, :, 1], 999.0))
                        g.sem_inc(s_const, 1)
                        g.dma_start(sorted_e.rearrange("(p t) f -> p t f", p=P), pad[:, :, :]).then_inc(s_padded, 16)
                        g.wait_ge(s_padded, 16)

                        def scatter(j, h, cols):
                            g.wait_ge(s_slot, j + 1)
                            g.sem_inc(s_pool, 1)
                            for k in range(cols):
                                g.indirect_dma_start(
                                    out=sorted_e[:, :], out_offset=bass.IndirectOffsetOnAxis(ap=dslot[h][:, k:k + 1], axis=0),
                                    in_=rslot[h][:, k, :], in_offset=None, bounds_check=P * NT - 1,
                                    oob_is_err=False).then_inc(s_scat[h], 16)
                        NS = EC // SC
                        assert EC % SC == 0 and NS % 2 == 0
                        with g.Fori(0, NS // 2) as j:
                            for h in range(2):
                                scatter(j * 2 + h, h, SC)
                        for h in range(2):
                            g.wait_ge(s_scat[h], NS // 2 * SC * 16)
                        g.dma_start(pad[:, :, :], sorted_e.rearrange("(p t) f -> p t f", p=P)).then_inc(s_back, 16)

                    @block.vector
                    def _(v):
                        v.wait_ge(s_const, 1)
                        v.wait_ge(s_in, 96)
                        link(v, v.tensor_copy(identb[:, :], ident[:, :]))
                        link(v, v.tensor_scalar(neg_ident[:, :], ident[:, :], NEG, None, ALU.mult))
                        link(v, v.tensor_scalar(kb_i[:, :], dst_i[:, :], 7, None, ALU.logical_shift_right))
                        link(v, v.tensor_scalar(ld_i[:, :], dst_i[:, :], P - 1, None, ALU.bitwise_and))
                        link(v, v.tensor_copy(kb[:, :], kb_i[:, :]))
                        link(v, v.tensor_copy(rec[:, :, 1], ld_i[:, :]))
                        link(v, v.tensor_copy(rec[:, :, 0], src_i[:, :]))
                        link(v, v.tensor_copy(rec[:, :, 3], w_in[:, :]))
                        link(v, v.memset(rank[:, :], 0.0))
                        with v.Fori(0, NB) as b:
                            v.tensor_scalar(eq[:, :], kb[:, :], bid[:, ds(b, 1)], None, ALU.is_equal).then_inc(s_eq, 1)
                            v.wait_ge(s_eq, b + 1)
                            v.tensor_tensor_scan(cnt[:, :], one_c[:, :], eq[:, :], 0.0, ALU.mult, ALU.add).then_inc(s_cnt, 1)
                            v.wait_ge(s_cnt, b + 1)
                            v.tensor_scalar(tot[:, ds(b, 1)], cnt[:, EC - 1:EC], 1.0, None, ALU.mult).then_inc(s_tot, 1)
                            v.tensor_tensor(eq[:, :], eq[:, :], cnt[:, :], ALU.mult).then_inc(s_mul, 1)
                            v.wait_ge(s_mul, b + 1)
                            v.tensor_tensor(rank[:, :], rank[:, :], eq[:, :], ALU.add).then_inc(s_rank, 1)
                            v.wait_ge(s_rank, b + 1)
                            v.wait_ge(s_tot, b + 1)
                        v.wait_ge(s_pre, 1)
                        pre, al = psG[:, 0:NB], psG[:, 64:64 + NB]
                        link(v, v.tensor_scalar(ngi[:, :], al, float(GE - 1), None, ALU.add))
                        link(v, v.tensor_scalar(kb_i[:, 0:NB], ngi[:, :], 8, None, ALU.logical_shift_right))
                        link(v, v.tensor_copy(ngr[:, 0, :], kb_i[:, 0:NB]))
                        gend = ngr[:, 1, :]
                        link(v, v.tensor_tensor_scan(gend, one_c[:, 0:NB], ngr[:, 0, :], 0.0, ALU.mult, ALU.add))
                        link(v, v.tensor_tensor(ngr[:, 2, :], gend, ngr[:, 0, :], ALU.subtract))
                        link(v, v.tensor_scalar(ngr[:, 3, :], ngr[:, 2, :], float(GE), -1.0, ALU.mult, ALU.add))
                        link(v, v.tensor_tensor(base[:, :], ngr[:, 3, :], pre, ALU.add))
                        with v.Fori(0, NB) as b:
                            v.tensor_scalar(eq[:, :], kb[:, :], bid[:, ds(b, 1)], base[:, ds(b, 1)],
                                            ALU.is_equal, ALU.mult).then_inc(s_eq, 1)
                            v.wait_ge(s_eq, b + (NB + 1))
                            v.tensor_tensor(rank[:, :], rank[:, :], eq[:, :], ALU.add).then_inc(s_rank, 1)
                            v.wait_ge(s_rank, b + (NB + 1))
                        link(v, v.tensor_copy(pos[:, :], rank[:, :]))
                        link(v, v.tensor_scalar(ld_i[:, :], pos[:, :], P - 1, None, ALU.bitwise_and))
                        link(v, v.tensor_scalar(kb_i[:, :], pos[:, :], 7, None, ALU.logical_shift_right))
                        link(v, v.tensor_copy(eq[:, :], ld_i[:, :]))
                        link(v, v.tensor_copy(cnt[:, :], kb_i[:, :]))
                        link(v, v.scalar_tensor_tensor(rank[:, :], eq[:, :], float(NT), cnt[:, :], ALU.mult, ALU.add))
                        link(v, v.tensor_scalar(eq[:, :], kb[:, :], float(NB), 1.0e6, ALU.is_ge, ALU.mult))
                        link(v, v.tensor_tensor(cnt[:, :], rank[:, :], eq[:, :], ALU.add))
                        link(v, v.tensor_scalar(cnt[:, :], cnt[:, :], 0.0, None, ALU.max))
                        link(v, v.tensor_copy(dest[:, :], cnt[:, :]))

                        def slots(j, h):
                            v.tensor_copy(rslot[h][:, :, :], rec[:, ds(j * SC, SC), :]).then_inc(s_mul, 1)
                            v.tensor_copy(dslot[h][:, :], dest[:, ds(j * SC, SC)]).then_inc(s_slot, 1)
                        for h in range(2):
                            slots(h, h)
                        with v.Fori(1, EC // SC // 2) as j:
                            for h in range(2):
                                v.wait_ge(s_scat[h], j * (SC * 16))
                                v.sem_inc(s_rec, 1)
                                slots(j * 2 + h, h)
                        link(v, v.tensor_tensor(jcmp[:, :, :], bc(jio[:, :], 2, NB), bc(gend[0:1, :], 1, NG), ALU.is_ge))
                        link(v, v.reduce_sum(jblk[:, :], jcmp[:, :, :], AX.X))
                        link(v, v.memset(blk[:, NG:], 0))
                        link(v, v.tensor_scalar(blk[:, 0:NG], jblk[:, :], float(NB - 1), None, ALU.min))
                        v.wait_ge(s_back, 16)
                        link(v, v.tensor_copy(e_src[:, :], pad[:, :, 0]))
                        link(v, v.tensor_copy(e_ld[:, :], pad[:, :, 1]))
                        link(v, v.tensor_copy(e_id[:, :], pad[:, :, 2]))
                        link(v, v.tensor_scalar(e_w[:, :], pad[:, :, 3], float(D) ** -0.5, None, ALU.mult))

                    @block.tensor
                    def _(pe):
                        pe.wait_ge(s_tot, NB)
                        pe.matmul(psG[:, 0:NB], tri[:, :], tot[:, :], start=True, stop=True)
                        pe.matmul(psG[:, 64:64 + NB], ones[:, :], tot[:, :], start=True, stop=True).then_inc(s_pre, 1)

        nm_in, nm_tr, nm_ev, nm_mm, nm_out = (sem(n) for n in ("nm_in", "nm_tr", "nm_ev", "nm_mm", "nm_out"))
        nm_base = [0]
        xs = [sb(f"xs{i}", [P, 256]) for i in range(2)]
        xT = [sb(f"xT{i}", [P, 2, P]) for i in range(2)]

        def node_matmul(src, K, W, cols, dst, bias=None):
            kt = K // P
            B = nm_base[0]
            nm_base[0] += NB

            def blocks(eng, step):
                step(0, 0)
                step(1, 1)
                pairs = (NB - 4) // 2 + 1
                with eng.Fori(1, pairs) as j:
                    step(j * 2, 0)
                    step(j * 2 + 1, 1)
                for b in range(2 * pairs, NB):
                    step(b, b % 2)

            def is_block(b, ahead):
                return not isinstance(b, int) or b + ahead < NB

            def w(eng, s, b, back):
                if not (isinstance(b, int) and b < back):
                    eng.wait_ge(s, b + (B + 1 - back))

            flat = lambda ap: ap.rearrange("p a c -> p (a c)")
            with nc.Block() as block:
                @block.vector
                def _(v):
                    def stage(b, s):
                        w(v, nm_tr, b, 2)
                        x = flat(src[:, ds(b, 1), :])
                        v.tensor_tensor(xs[s][:, 0:K], x, x, ALU.max).then_inc(nm_in, 1)

                    def step(b, s):
                        if is_block(b, 2):
                            stage(b + 2, s)
                        w(v, nm_mm, b, 0)
                        y = flat(dst[:, ds(b, 1), 0:cols])
                        if bias is not None:
                            ins = v.tensor_tensor(y, psS[s][:, 0:cols], bias, ALU.add)
                        else:
                            ins = v.tensor_scalar(y, psS[s][:, 0:cols], 0.0, None, ALU.add)
                        ins.then_inc(nm_out, 1)
                    stage(0, 0)
                    stage(1, 1)
                    blocks(v, step)

                @block.tensor
                def _(pe):
                    def tr(b, s):
                        w(pe, nm_in, b, 0)
                        w(pe, nm_ev, b, 2)
                        for k in range(kt):
                            ins = pe.transpose(psM[s][:, k, 0:P], xs[s][:, k * P:(k + 1) * P], ident[:, :])
                        ins.then_inc(nm_tr, 1)

                    def mm(b, s):
                        w(pe, nm_ev, b, 0)
                        w(pe, nm_out, b, 2)
                        for k in range(kt):
                            ins = pe.matmul(psS[s][:, 0:cols], xT[s][:, k, :], W[:, k, 0:cols],
                                            start=(k == 0), stop=(k == kt - 1))
                        ins.then_inc(nm_mm, 1)

                    def step(b, s):
                        if is_block(b, 1):
                            tr(b + 1, 1 - s)
                        mm(b, s)
                    tr(0, 0)
                    blocks(pe, step)

                @block.scalar
                def _(a):
                    def step(b, s):
                        w(a, nm_tr, b, 0)
                        w(a, nm_mm, b, 2)
                        a.activation(xT[s][:, 0:kt, :], psM[s][:, 0:kt, 0:P], ACT.Copy).then_inc(nm_ev, 1)
                    blocks(a, step)

        s_half = sem("s_half")
        halves = [0]

        def vector_act_vector(before, act_step, after):
            halves[0] += 2
            mark = halves[0]
            with nc.Block() as block:
                @block.vector
                def _(v):
                    before(v)
                    v.nop().then_inc(s_half, 1)
                    if after:
                        v.wait_ge(s_half, mark)
                        after(v)

                @block.scalar
                def _(a):
                    a.wait_ge(s_half, mark - 1)
                    act_step(a).then_inc(s_half, 1)

        ne_ready, p1_done, ev_done, p2_done, gm_done, t_done, t2_done, mn_done, d_done, m_done = (
            sem(n) for n in ("not_dst_ready", "transposed", "evacuated", "masked_ready", "tile_max_ready", "max_plus_dst",
                             "leaky_max_ready", "new_max_ready", "max_step_ready", "max_stored"))
        p3_done, z1_done, z2_done, z3_done, ex_done, hx_done, sg_done, sc_done, as_done, ac_done = (
            sem(n) for n in ("dst_terms_ready", "logit_sum", "logit_leaky", "logit_shifted", "exp_ready", "weighted_ready",
                             "segsum_ready", "rescale_ready", "acc_rescaled", "acc_added"))
        gathered = [sem(f"gathered{i}") for i in range(UN)]
        idx_ready = sem("idx_ready")
        go = sem("go")
        base = {"group": {}, "gathered": 0, "idx_ready": 0}

        def counts(n_src):
            mine = {}
            landed = TG * n_src * 16
            GB = base["gathered"]
            marks = base["idx_ready"]

            def start(s, per):
                if s.name not in mine:
                    mine[s.name] = base["group"].get(s.name, 0)
                    base["group"][s.name] = mine[s.name] + NG * per
                return mine[s.name]

            def w(eng, s, g, back=0, per=1):
                B = start(s, per)
                if isinstance(g, int) and g < back:
                    return
                eng.wait_ge(s, g * per + (B + (1 - back) * per))

            def rows_in(eng, g, slot):
                if isinstance(g, int):
                    eng.wait_ge(gathered[slot], GB + (g // UN + 1) * landed)
                else:
                    eng.wait_ge(gathered[slot], g * (landed // UN) + (GB + landed - slot * (landed // UN)))
            base["gathered"] += NG // UN * landed
            base["idx_ready"] += NG // IG * n_src
            return w, rows_in, start, marks

        def stage_indices(a, sources, j, half):
            for q, (table, indices, dst, width) in enumerate(sources):
                a.activation(idx[half][:, q, :], indices[:, ds(j * (IG * TG), IG * TG)], ACT.Copy).then_inc(idx_ready, 1)

        def stage_when_due(a, sources, g, s, ahead):
            if (s + ahead + 5) % IG == 0 and g_in(g, ahead + 5):
                first = g + (ahead + 5)
                for q, (table, indices, dst, width) in enumerate(sources):
                    a.activation(idx[(s + ahead + 5) // IG % 2][:, q, :], indices[:, ds(first * TG, IG * TG)],
                                 ACT.Copy).then_inc(idx_ready, 1)

        def gathers(block, sources, consumed, start, marks, weigh=None):
            n_src = len(sources)
            B, IB = start(consumed, 1), marks

            @block.gpsimd
            def _(g):
                def body(j, first):
                    for half in range(2):
                        jj = j * 2 + half
                        g.wait_ge(idx_ready, jj * n_src + (IB + n_src))
                        g.sem_inc(go, 1)
                        for r in range(IG):
                            if weigh and not (first and half * IG + r < UN - 1):
                                weigh(g, jj * IG + (r + 1 - UN), (half * IG + r + 1) % UN)
                            if not first:
                                g.wait_ge(consumed, jj * IG + (B + r + 1 - UN))
                                g.sem_inc(go, 1)
                            for t in range(TG):
                                for q, (table, indices, dst, width) in enumerate(sources):
                                    g.indirect_dma_start(
                                        out=dst[half * IG + r][:, t, 0:width], out_offset=None, in_=table,
                                        in_offset=bass.IndirectOffsetOnAxis(
                                            ap=idx[half][:, q, r * TG + t:r * TG + t + 1], axis=0)).then_inc(gathered[half * IG + r], 16)
                body(0, True)
                with g.Fori(1, NG // UN) as j:
                    body(j, False)
                if weigh:
                    for r in range(NG + 1 - UN, NG):
                        weigh(g, r, r % UN)

        def gat_edges(table, C, Hn):
            W1c = C + 1
            RW = Hn * W1c
            RT = RW + (3 * Hn + 1) // 2
            w, rows_in, start, marks = counts(1)
            sel = head_sel if Hn == 4 else head_sel1
            H4 = [h[:, :, 0:RW].rearrange("p t (h c) -> p t h c", h=Hn) for h in H]
            Hx4 = [h[:, :, 0:RW].rearrange("p t (h c) -> p t h c", h=Hn) for h in Hx]
            AS = [[h[:, t, RW:RT].bitcast(bf16)[:, 0:3 * Hn] for t in range(TG)] for h in H]
            acc4 = lambda b: acc[:, ds(b, 1), 0:RW].rearrange("p a (h c) -> p (a h) c", h=Hn)
            Vb = lambda b: V[:, ds(b, 1), :].rearrange("p a c -> p (a c)")
            G = [psG[:, 16 * i:16 * i + 16].rearrange("p (t c) -> p t c", t=TG) for i in range(2)]

            def weigh(g, group, s):
                w(g, ex_done, group)
                g.sem_inc(go, 1)
                x = Hx4[s % 4]
                g.tensor_tensor(x[:, :, :, 0:C], H4[s][:, :, :, 0:C],
                                x[:, :, :, C:C + 1].to_broadcast([P, TG, Hn, C]), ALU.mult).then_inc(hx_done, 1)

            with nc.Block() as block:
                sources = [(table[:, :], e_src, H, RT)]
                gathers(block, sources, hx_done, start, marks, weigh)

                @block.vector
                def _(v):
                    def not_dst(g, s):
                        v.tensor_tensor(NE[s][:, :, :], bc(iota_row[:, :], 1, TG), bc(e_ld[:, ds(g * TG, TG)], 2, P),
                                        ALU.not_equal).then_inc(ne_ready, 1)

                    def tile_max(g, s):
                        w(v, p2_done, g)
                        w(v, t_done, g, 1)
                        v.tensor_reduce(gm[:, 0:Hn], psM[s % 2][:, :, 0:Hn * P].rearrange("p t (h e) -> p h t e", h=Hn),
                                        AX.XY, ALU.max).then_inc(gm_done, 1)

                    def step(g, s, block_of):
                        hot, top, logit, add = (g_in(g, a) for a in (2, 0, -1, -5))
                        k, k5 = (s - 1) % UN, (s - 5) % UN
                        i1 = (s - 1) % 2
                        if top:
                            b = block_of(0)
                        if logit:
                            w(v, p3_done, g - 1)
                            v.tensor_tensor(z[k][:, :, 0:Hn], G[i1][:, :, 0:Hn], H4[k][:, :, :, C], ALU.add).then_inc(z1_done, 1)
                        if hot:
                            not_dst(g + 2, (s + 2) % UN)
                        if top:
                            w(v, gm_done, g)
                            v.tensor_tensor(tm[:, 0:Hn], gm[:, 0:Hn], Vb(b)[:, 0:Hn], ALU.add).then_inc(t_done, 1)
                        if logit:
                            w(v, z1_done, g - 1)
                            v.scalar_tensor_tensor(z[k][:, :, 0:Hn], z[k][:, :, 0:Hn], SLOPE, z[k][:, :, 0:Hn],
                                                   ALU.mult, ALU.max).then_inc(z2_done, 1)
                        if top:
                            w(v, t_done, g)
                            v.scalar_tensor_tensor(tm[:, 0:Hn], tm[:, 0:Hn], SLOPE, tm[:, 0:Hn], ALU.mult, ALU.max).then_inc(t2_done, 1)
                        if logit:
                            w(v, z2_done, g - 1)
                            v.tensor_tensor(z[k][:, :, 0:Hn], z[k][:, :, 0:Hn], G[i1][:, :, 4:4 + Hn],
                                            ALU.subtract).then_inc(z3_done, 1)
                        if add:
                            b5 = block_of(-5)
                            w(v, sc_done, g - 5)
                            w(v, ac_done, g - 5, 1)
                            sums = psS[k5 % 2][:, 0:RW].rearrange("p (h c) -> p h c", h=Hn)
                            if Hn > 1:
                                v.tensor_tensor(acc4(b5), acc4(b5), bc(sc[k5][:, 0:Hn], 2, W1c), ALU.mult).then_inc(as_done, 1)
                        if top:
                            w(v, t2_done, g)
                            v.tensor_tensor(mn[:, 0:Hn], tm[:, 0:Hn], Vb(b)[:, 4:4 + Hn], ALU.max).then_inc(mn_done, 1)
                        if add:
                            w(v, sg_done, g - 5)
                            if Hn > 1:
                                w(v, as_done, g - 5)
                                v.tensor_tensor(acc4(b5), acc4(b5), sums, ALU.add).then_inc(ac_done, 1)
                            else:
                                v.scalar_tensor_tensor(acc4(b5), acc4(b5), sc[k5][:, 0:1], sums, ALU.mult,
                                                       ALU.add).then_inc(ac_done, 1)
                        if top:
                            w(v, mn_done, g)
                            v.tensor_tensor(dm[s][:, 0:Hn], Vb(b)[:, 4:4 + Hn], mn[:, 0:Hn], ALU.subtract).then_inc(d_done, 1)
                            w(v, d_done, g)
                            v.tensor_tensor(Vb(b)[:, 4:4 + Hn], mn[:, 0:Hn], mn[:, 0:Hn], ALU.max).then_inc(m_done, 1)
                        if g_in(g, 1):
                            tile_max(g + 1, (s + 1) % UN)
                    for g in range(2):
                        not_dst(g, g)
                    tile_max(0, 0)
                    pipeline(nc, blk, v, step, NG + 5, lo=-8)

                @block.tensor
                def _(pe):
                    def transposes(g, s):
                        w(pe, ne_ready, g)
                        rows_in(pe, g, s)
                        w(pe, ev_done, g, 1)
                        for t in range(TG):
                            pe.transpose(psTb[:, t * P:(t + 1) * P], NE[s][:, t, :], identb[:, :])
                        for t in range(TG):
                            ins = pe.matmul(psT[0:3 * Hn, (TG + t) * P:(TG + t + 1) * P], AS[s][t], identb[:, :],
                                            start=True, stop=True)
                        ins.then_inc(p1_done, 1)

                    def masked(g, s):
                        i = s % 2
                        w(pe, ev_done, g)
                        for t in range(TG):
                            pe.matmul(psM[i][:, t, 0:Hn * P].rearrange("p (h e) -> p h e", h=Hn), NE[s][:, t, :],
                                      bc(neg_ident[:, :], 1, Hn), start=True, stop=False)
                            for h in range(Hn):
                                ins = pe.matmul(psM[i][:, t, h * P:(h + 1) * P], sel[:, h, :], asT[s % 4][0:3 * Hn, t, :],
                                                start=False, stop=(h == Hn - 1))
                        ins.then_inc(p2_done, 1)

                    def dst_terms(g, s, b):
                        i = s % 2
                        w(pe, m_done, g)
                        for t in range(TG):
                            ins = pe.matmul(G[i][:, t, :], OT[s][:, t, :], Vb(b), start=True, stop=True)
                        ins.then_inc(p3_done, 1)

                    def segment_sum(g, s):
                        w(pe, hx_done, g)
                        w(pe, ac_done, g, 2)
                        for t in range(TG):
                            ins = pe.matmul(psS[s % 2][:, 0:RW], O[s][:, t, :], Hx[s % 4][:, t, 0:RW], start=(t == 0),
                                            stop=(t == TG - 1))
                        ins.then_inc(sg_done, 1)

                    def step(g, s, block_of):
                        if g_in(g, -1):
                            dst_terms(g - 1, (s - 1) % UN, block_of(-1))
                        if g_in(g, -5):
                            segment_sum(g - 5, (s - 5) % UN)
                        if g_in(g, 1):
                            masked(g + 1, (s + 1) % UN)
                        if g_in(g, 2):
                            transposes(g + 2, (s + 2) % UN)
                    transposes(0, 0)
                    transposes(1, 1)
                    masked(0, 0)
                    pipeline(nc, blk, pe, step, NG + 5, lo=-4)

                @block.scalar
                def _(a):
                    def evacuate(g, s):
                        w(a, ne_ready, g)
                        a.activation(O[s][:, :, :], NE[s][:, :, :], ACT.Identity, scale=-1.0, bias=ones[:, 0:1])
                        w(a, p1_done, g)
                        a.activation(OT[s][:, :, :], psTb[:, 0:TG * P].rearrange("p (t e) -> p t e", t=TG),
                                     ACT.Identity, scale=-1.0, bias=ones[:, 0:1])
                        a.activation(asT[s % 4][0:3 * Hn, :, :],
                                     psT[0:3 * Hn, TG * P:2 * TG * P].rearrange("p (t e) -> p t e", t=TG),
                                     ACT.Copy).then_inc(ev_done, 1)

                    def exps(g, s):
                        w(a, z3_done, g)
                        w(a, sg_done, g, 4)
                        a.activation(Hx4[s % 4][:, :, :, C], z[s][:, :, 0:Hn], ACT.Exp).then_inc(ex_done, 1)

                    def rescale(g, s):
                        w(a, d_done, g)
                        a.activation(sc[s][:, 0:Hn], dm[s][:, 0:Hn], ACT.Exp).then_inc(sc_done, 1)

                    def step(g, s, block_of):
                        if g_in(g, 2):
                            evacuate(g + 2, (s + 2) % UN)
                            stage_when_due(a, sources, g, s, 2)
                        if g_in(g, -1):
                            exps(g - 1, (s - 1) % UN)
                        if g_in(g, 0):
                            rescale(g, s)
                    stage_indices(a, sources, 0, 0)
                    stage_indices(a, sources, 1, 1)
                    evacuate(0, 0)
                    evacuate(1, 1)
                    pipeline(nc, blk, a, step, NG + 1)

        pj_done, gl_done, at1, at2, at_done = (sem(n) for n in (
            "projected", "gelu_ready", "dot_ready", "dot_bias_ready", "attn_ready"))

        def edge_attention(table, ev):
            w, rows_in, start, marks = counts(2)
            pE = [psM[0][:, i, 0:TG * D].rearrange("p (t c) -> p t c", t=TG) for i in range(2)]
            pQ = [psM[1][:, i, 0:TG * (D + 1)].rearrange("p (t c) -> p t c", t=TG) for i in range(2)]
            pA = [m[:, TG * D:2 * TG * D].rearrange("p (t c) -> p t c", t=TG) for m in psS]
            G = [psG[:, 16 * i:16 * i + TG] for i in range(2)]
            V0 = lambda b: V[:, ds(b, 1), 0:1].rearrange("p a c -> p (a c)")
            accb = lambda b: acc[:, ds(b, 1), 0:D + 1].rearrange("p a c -> p (a c)")
            with nc.Block() as block:
                sources = [(table[:, :], e_src, H, D), (ev, e_id, EV, D)]
                gathers(block, sources, pj_done, start, marks)

                @block.vector
                def _(v):
                    def not_dst(g, s):
                        v.tensor_tensor(NE[s][:, :, :], bc(iota_row[:, :], 1, TG), bc(e_ld[:, ds(g * TG, TG)], 2, P),
                                        ALU.not_equal).then_inc(ne_ready, 1)

                    def step(g, s, block_of):
                        s1, s2, s3, s5 = (s - 1) % UN, (s - 2) % UN, (s - 3) % UN, (s - 5) % UN
                        hot, dot, top, shift, wgt, add = (g_in(g, a) for a in (3, 0, -1, -2, -3, -5))
                        if dot:
                            w(v, gl_done, g)
                            for t in range(TG):
                                v.tensor_tensor_reduce(junk[:, t, :], Tt[s][:, t, :], pQ[s % 2][:, t, 0:D], 1.0, 0.0, ALU.mult,
                                                       ALU.add, accum_out=attn[s][:, t:t + 1]).then_inc(at1, 1)
                        if top:
                            b = block_of(-1)
                            w(v, p2_done, g - 1)
                            v.tensor_reduce(gm[:, 0:1], pA[s1 % 2], AX.XY, ALU.max).then_inc(gm_done, 1)
                        if dot:
                            w(v, at1, g, 0, TG)
                            v.tensor_tensor(attn[s][:, :], attn[s][:, :], pQ[s % 2][:, :, D], ALU.add).then_inc(at2, 1)
                        if shift:
                            w(v, p3_done, g - 2)
                            v.tensor_tensor(z[s2][:, :, 0], attn[s2][:, :], G[s2 % 2], ALU.subtract).then_inc(z3_done, 1)
                        if dot:
                            w(v, at2, g)
                            v.tensor_tensor(attn[s][:, :], attn[s][:, :], e_w[:, ds(g * TG, TG)], ALU.mult).then_inc(at_done, 1)
                        if top:
                            w(v, gm_done, g - 1)
                            v.tensor_tensor(mn[:, 0:1], gm[:, 0:1], V0(b), ALU.max).then_inc(mn_done, 1)
                        if top:
                            w(v, mn_done, g - 1)
                            v.tensor_tensor(dm[s1][:, 0:1], V0(b), mn[:, 0:1], ALU.subtract).then_inc(d_done, 1)
                        if add:
                            b5 = block_of(-5)
                            w(v, sc_done, g - 5)
                            w(v, sg_done, g - 5)
                            w(v, ac_done, g - 5, 1)
                            v.scalar_tensor_tensor(accb(b5), accb(b5), sc[s5][:, 0:1], psS[s5 % 2][:, 0:D + 1], ALU.mult,
                                                   ALU.add).then_inc(ac_done, 1)
                        if hot:
                            not_dst(g + 3, (s + 3) % UN)
                        if top:
                            w(v, d_done, g - 1)
                            v.tensor_tensor(V0(b), mn[:, 0:1], mn[:, 0:1], ALU.max).then_inc(m_done, 1)
                        if wgt:
                            w(v, ex_done, g - 3)
                            x = Hx[s3 % 4]
                            v.tensor_tensor(x[:, :, 0:D], Tt[s3][:, :, :], x[:, :, D:D + 1].to_broadcast([P, TG, D]),
                                            ALU.mult).then_inc(hx_done, 1)
                    for g in range(3):
                        not_dst(g, g)
                    pipeline(nc, blk, v, step, NG + 5, lo=-8)

                @block.tensor
                def _(pe):
                    def transposes(g, s):
                        w(pe, ne_ready, g)
                        rows_in(pe, g, s)
                        w(pe, ev_done, g, 1)
                        for t in range(TG):
                            pe.transpose(psTb[:, t * P:(t + 1) * P], NE[s][:, t, :], identb[:, :])
                        for t in range(TG):
                            ins = pe.transpose(psT[:, (TG + t) * P:(TG + t + 1) * P], EV[s][:, t, :], ident[:, :])
                        ins.then_inc(p1_done, 1)

                    def project(g, s, b):
                        i = s % 2
                        w(pe, ev_done, g)
                        w(pe, gl_done, g, 2)
                        w(pe, at2, g, 2)
                        for t in range(TG):
                            pe.matmul(pE[i][:, t, :], evT[s % 4][:, t, :], WT2[:, :], start=True, stop=False)
                            pe.matmul(pE[i][:, t, :], ident[:, :], H[s][:, t, 0:D], start=False, stop=True)
                            ins = pe.matmul(pQ[i][:, t, :], OT[s][:, t, :], QK[:, ds(b, 1), :].rearrange("p a c -> p (a c)"),
                                            start=True, stop=True)
                        ins.then_inc(pj_done, 1)

                    def masked(g, s):
                        i = s % 2
                        w(pe, at_done, g)
                        for t in range(TG):
                            pe.matmul(pA[i][:, t, :], NE[s][:, t, :], neg_ident[:, :], start=True, stop=False)
                            ins = pe.matmul(pA[i][:, t, :], attn[s][:, t:t + 1].to_broadcast([P, P]), ident[:, :],
                                            start=False, stop=True)
                        ins.then_inc(p2_done, 1)

                    def dst_max(g, s, b):
                        w(pe, m_done, g)
                        for t in range(TG):
                            ins = pe.matmul(G[s % 2][:, t:t + 1], OT[s][:, t, :], V0(b), start=True, stop=True)
                        ins.then_inc(p3_done, 1)

                    def segment_sum(g, s):
                        w(pe, hx_done, g)
                        for t in range(TG):
                            ins = pe.matmul(psS[s % 2][:, 0:D + 1], O[s][:, t, :], Hx[s % 4][:, t, 0:D + 1], start=(t == 0),
                                            stop=(t == TG - 1))
                        ins.then_inc(sg_done, 1)

                    def step(g, s, block_of):
                        if g_in(g, 2):
                            project(g + 2, (s + 2) % UN, block_of(2))
                        if g_in(g, 3):
                            transposes(g + 3, (s + 3) % UN)
                        if g_in(g, -4):
                            segment_sum(g - 4, (s - 4) % UN)
                        if g_in(g, 0):
                            masked(g, s)
                        if g_in(g, -1):
                            dst_max(g - 1, (s - 1) % UN, block_of(-1))
                    transposes(0, 0)
                    transposes(1, 1)
                    transposes(2, 2)
                    for g in range(2):
                        project(g, g, pe.value_load(blk[0:1, g:g + 1], min_val=0, max_val=NB - 1))
                    pipeline(nc, blk, pe, step, NG + 4, lo=-4, hi=4)

                @block.scalar
                def _(a):
                    def evacuate(g, s):
                        w(a, ne_ready, g)
                        a.activation(O[s][:, :, :], NE[s][:, :, :], ACT.Identity, scale=-1.0, bias=ones[:, 0:1])
                        w(a, p1_done, g)
                        a.activation(OT[s][:, :, :], psTb[:, 0:TG * P].rearrange("p (t e) -> p t e", t=TG),
                                     ACT.Identity, scale=-1.0, bias=ones[:, 0:1])
                        a.activation(evT[s % 4][:, :, :], psT[:, TG * P:2 * TG * P].rearrange("p (t e) -> p t e", t=TG),
                                     ACT.Copy).then_inc(ev_done, 1)

                    def gelu(g, s):
                        w(a, pj_done, g)
                        a.activation(Tt[s][:, :, :], pE[s % 2], ACT.Gelu).then_inc(gl_done, 1)

                    def exps(g, s):
                        w(a, z3_done, g)
                        a.activation(Hx[s % 4][:, :, D], z[s][:, :, 0], ACT.Exp).then_inc(ex_done, 1)

                    def rescale(g, s):
                        w(a, d_done, g)
                        a.activation(sc[s][:, 0:1], dm[s][:, 0:1], ACT.Exp).then_inc(sc_done, 1)

                    def step(g, s, block_of):
                        if s % 2:
                            for back in (3, 2):
                                if g_in(g, -back):
                                    exps(g - back, (s - back) % UN)
                                    rescale(g - back, (s - back) % UN)
                            for ahead in (1, 2):
                                if g_in(g, ahead):
                                    gelu(g + ahead, (s + ahead) % UN)
                        if g_in(g, 3):
                            evacuate(g + 3, (s + 3) % UN)
                            stage_when_due(a, sources, g, s, 3)
                    stage_indices(a, sources, 0, 0)
                    stage_indices(a, sources, 1, 1)
                    for g in range(3):
                        evacuate(g, g)
                    for g in range(2):
                        gelu(g, g)
                    pipeline(nc, blk, a, step, NG + 2)

        def edge_sums(table):
            w, rows_in, start, marks = counts(1)
            accb = lambda b: acc[:, ds(b, 1), 0:D].rearrange("p a c -> p (a c)")
            with nc.Block() as block:
                sources = [(table[:, :], e_src, H, D)]
                gathers(block, sources, sg_done, start, marks)

                @block.vector
                def _(v):
                    def onehot(g, s):
                        for t in range(TG):
                            ins = v.tensor_scalar(O[s][:, t, :], iota_row[:, :], e_ld[:, ds(g * TG + t, 1)], None, ALU.is_equal)
                        ins.then_inc(ne_ready, 1)

                    def accumulate(g, s, b):
                        w(v, ac_done, g, 1)
                        w(v, sg_done, g)
                        v.tensor_tensor(accb(b), accb(b), psS[s % 2][:, 0:D], ALU.add).then_inc(ac_done, 1)

                    def step(g, s, block_of):
                        if g_in(g, 2):
                            onehot(g + 2, (s + 2) % UN)
                        if g_in(g, -1):
                            accumulate(g - 1, (s - 1) % UN, block_of(-1))
                    onehot(0, 0)
                    onehot(1, 1)
                    pipeline(nc, blk, v, step, NG + 1, lo=-4)

                @block.tensor
                def _(pe):
                    def step(g, s, block_of):
                        w(pe, ne_ready, g)
                        rows_in(pe, g, s)
                        w(pe, ac_done, g, 2)
                        for t in range(TG):
                            ins = pe.matmul(psS[s % 2][:, 0:D], O[s][:, t, :], H[s][:, t, 0:D], start=(t == 0), stop=(t == TG - 1))
                        ins.then_inc(sg_done, 1)
                    pipeline(nc, blk, pe, step, NG)

                @block.scalar
                def _(a):
                    def step(g, s, block_of):
                        if g_in(g, 5) and (s + 5) % IG == 0:
                            w(a, sg_done, g)
                            a.sem_inc(go, 1)
                            stage_when_due(a, sources, g, s, 0)
                    stage_indices(a, sources, 0, 0)
                    stage_indices(a, sources, 1, 1)
                    pipeline(nc, blk, a, step, NG)

        def loads_of(pairs):
            with nc.Block() as block:
                @block.sync
                def _(sp):
                    for dst, src in pairs:
                        load(sp, dst, src)
                    loaded(sp)

        def vector_part(program):
            with nc.Block() as block:
                @block.vector
                def _(v):
                    program(v)

        def store_table(table, cols):
            with nc.Block() as block:
                @block.sync
                def _(sp):
                    load(sp, table.rearrange("(b p) c -> p b c", p=P), Z[:, :, 0:cols])
                    loaded(sp)

        def head_rows(ap, C, Hn):
            return ap[:, :, 0:Hn * (C + 1)].rearrange("p b (h c) -> p b h c", h=Hn)

        def denominators(v, den, Hn):
            r = small[:, 0, 0:NB * Hn].rearrange("p (b h) -> p b h", h=Hn)
            link(v, v.tensor_scalar(r, den, EPS_SM, None, ALU.add))
            link(v, v.reciprocal(r, r))
            return r

        def row(i, cols):
            return bc(brow[:, i, 0:cols], 1, NB)

        def layernorm_into(src, dst, tmp, gamma=None, beta=None):
            mean, var = small[:, 1, 0:NB], small[:, 2, 0:NB]

            def before(v):
                link(v, v.reduce_sum(mean, src, AX.X))
                link(v, v.tensor_scalar(mean, mean, 1.0 / D, None, ALU.mult))
                link(v, v.tensor_tensor(src, src, bc(mean, 2, D), ALU.subtract))
                link(v, v.tensor_tensor(tmp, src, src, ALU.mult))
                link(v, v.reduce_sum(var, tmp, AX.X))
                link(v, v.tensor_scalar(var, var, 1.0 / D, EPS_LN, ALU.mult, ALU.add))

            def after(v):
                link(v, v.reciprocal(var, var))
                link(v, v.tensor_tensor(dst, src, bc(var, 2, D), ALU.mult))
                if gamma is not None:
                    link(v, v.tensor_tensor(dst, dst, gamma, ALU.mult))
                    link(v, v.tensor_tensor(dst, dst, beta, ALU.add))
            vector_act_vector(before, lambda a: a.activation(var, var, ACT.Sqrt), after)

        def gat_layer(name, src, K, W, a_s, a_d, b, C, Hn, own_edge=False):
            kt = K // P
            HC, RW = Hn * C, Hn * (C + 1)
            RT = RW + (3 * Hn + 1) // 2
            table = nc.dram_tensor(f"table_{name}", [NB * P, RT], f32).ap()
            loads_of([(WR[:, 0:kt, 0:HC], W.rearrange("(k p) n -> p k n", p=P)),
                      (vec[:, 0, 0:HC], rows(a_s.rearrange("h c -> (h c)"))),
                      (vec[:, 1, 0:HC], rows(a_d.rearrange("h c -> (h c)"))),
                      (brow[:, 0, 0:HC], rows(b))])

            def weights(v):
                hc = lambda ap: ap.rearrange("p (h c) -> p h c", h=Hn)
                for k in range(kt):
                    own = WA[:, k, 0:RW].rearrange("p (h c) -> p h c", h=Hn)
                    link(v, v.tensor_copy(own[:, :, 0:C], hc(WR[:, k, 0:HC])))
                    link(v, v.tensor_tensor(wtmp[:, 0:HC], WR[:, k, 0:HC], vec[:, 0, 0:HC], ALU.mult))
                    link(v, v.reduce_sum(own[:, :, C], hc(wtmp[:, 0:HC]), AX.X))
                    link(v, v.tensor_tensor(wtmp[:, 0:HC], WR[:, k, 0:HC], vec[:, 1, 0:HC], ALU.mult))
                    link(v, v.reduce_sum(WA[:, k, RW:RW + Hn], hc(wtmp[:, 0:HC]), AX.X))
            vector_part(weights)
            node_matmul(src, K, WA, RW + Hn, Z)

            def tables(v):
                link(v, v.memset(V[:, :, :], NEG))
                link(v, v.tensor_copy(V[:, :, 0:Hn], Z[:, :, RW:RW + Hn]))
                a_src = head_rows(Z, C, Hn)[:, :, :, C]
                if own_edge:
                    top = V[:, :, 4:4 + Hn]
                    link(v, v.tensor_tensor(top, a_src, V[:, :, 0:Hn], ALU.add))
                    link(v, v.scalar_tensor_tensor(top, top, SLOPE, top, ALU.mult, ALU.max))
                    link(v, v.tensor_copy(acc[:, :, 0:RW], Z[:, :, 0:RW]))
                    link(v, v.memset(head_rows(acc, C, Hn)[:, :, :, C], 1.0))
                else:
                    link(v, v.memset(acc[:, :, 0:RW], 0.0))
                link(v, v.memset(Z[:, :, RW:RT], 0.0))
                parts = Z[:, :, RW:RT].bitcast(bf16)
                rest = small[:, 3, 0:NB * Hn].rearrange("p (b h) -> p b h", h=Hn)
                pt = lambda q: parts[:, :, q:q + 3 * (Hn - 1) + 1:3] if Hn > 1 else parts[:, :, q:q + 1]
                link(v, v.tensor_copy(pt(0), a_src))
                link(v, v.tensor_tensor(rest, a_src, pt(0), ALU.subtract))
                link(v, v.tensor_copy(pt(1), rest))
                link(v, v.tensor_tensor(rest, rest, pt(1), ALU.subtract))
                link(v, v.tensor_copy(pt(2), rest))
            vector_part(tables)
            store_table(table, RT)
            gat_edges(table, C, Hn)

        def heads_out(v, dst, C, Hn):
            a4 = head_rows(acc, C, Hn)
            r = denominators(v, a4[:, :, :, C], Hn)
            link(v, v.tensor_tensor(dst.rearrange("p b (h c) -> p b h c", h=Hn), a4[:, :, :, 0:C], bc(r, 3, C), ALU.mult))
            link(v, v.tensor_tensor(dst, dst, row(0, Hn * C), ALU.add))

        def elu_out():
            def before(v):
                heads_out(v, Y[:, :, :], 64, 4)
                link(v, v.tensor_scalar(Z[:, :, 0:256], Y[:, :, :], 0.0, None, ALU.min))

            def after(v):
                link(v, v.scalar_tensor_tensor(Y[:, :, :], Y[:, :, :], 0.0, Z[:, :, 0:256], ALU.max, ALU.add))
                link(v, v.tensor_scalar(Y[:, :, :], Y[:, :, :], 1.0, None, ALU.subtract))
            vector_act_vector(before, lambda a: a.activation(Z[:, :, 0:256], Z[:, :, 0:256], ACT.Exp), after)

        def add_norm(src):
            vector_part(lambda v: link(v, v.tensor_tensor(X[:, :, :], X[:, :, :], src, ALU.add)))
            layernorm_into(X[:, :, :], X[:, :, :], Z[:, :, 0:D])

        def transposed_weight(dst):
            halves[0] += 1
            mark = halves[0]
            with nc.Block() as block:
                @block.tensor
                def _(pe):
                    pe.transpose(psS[0][:, 0:P], WR[:, 0, 0:D], ident[:, :]).then_inc(s_half, 1)

                @block.vector
                def _(v):
                    v.wait_ge(s_half, mark)
                    link(v, v.tensor_copy(dst, psS[0][:, 0:P]))

        Yl, Yr = Y[:, :, 0:D], Y[:, :, D:2 * D]

        def finish(src):
            with nc.Block() as block:
                @block.sync
                def _(sp):
                    load(sp, out[0:(NB - 1) * P, :].rearrange("(b p) c -> p b c", p=P), src[:, 0:NB - 1, :])
                    load(sp, out[(NB - 1) * P:N, :], src[0:LASTN, NB - 1, :])
                    loaded(sp)

        def read_x():
            x = T["x"]
            vector_part(lambda v: link(v, v.memset(X[:, NB - 1, :], 0.0)))
            loads_of([(X[:, 0:NB - 1, :], x[0:(NB - 1) * P, :].rearrange("(b p) c -> p b c", p=P)),
                      (X[0:LASTN, NB - 1, :], x[(NB - 1) * P:N, :])])

        setup()
        read_x()
        gat_layer("l0a", X[:, :, :], D, T["L0_gnn_W0"], T["L0_gnn_as0"], T["L0_gnn_ad0"], T["L0_gnn_b0"], 64, 4, own_edge=True)
        elu_out()
        if stop == "l0a":
            return finish(Yl)
        gat_layer("l0b", Y[:, :, :], 256, T["L0_gnn_W1"], T["L0_gnn_as1"], T["L0_gnn_ad1"], T["L0_gnn_b1"], 64, 4, own_edge=True)
        elu_out()
        gat_layer("l0c", Y[:, :, :], 256, T["L0_gnn_W2"], T["L0_gnn_as2"], T["L0_gnn_ad2"], T["L0_gnn_b2"], 128, 1, own_edge=True)
        vector_part(lambda v: heads_out(v, Yl, 128, 1))
        add_norm(Yl)
        if stop == "l0":
            return finish(X)

        gat_layer("l1a", X[:, :, :], D, T["L1_gnn_W0"], T["L1_gnn_att_src0"], T["L1_gnn_att_dst0"], T["L1_gnn_b0"], 32, 4)

        def relu_out(v):
            heads_out(v, Yl, 32, 4)
            link(v, v.tensor_scalar(Yl, Yl, 0.0, None, ALU.max))
        vector_part(relu_out)
        gat_layer("l1b", Yl, D, T["L1_gnn_W1"], T["L1_gnn_att_src1"], T["L1_gnn_att_dst1"], T["L1_gnn_b1"], 32, 4)
        vector_part(lambda v: heads_out(v, Yl, 32, 4))
        add_norm(Yl)
        if stop == "l1":
            return finish(X)

        Wt = T["L2_gnn_Wt"]
        loads_of([(brow[:, 0, 0:D], rows(T["L2_gnn_gamma"])), (brow[:, 1, 0:D], rows(T["L2_gnn_beta"])),
                  (brow[:, 2, 0:D], rows(T["L2_gnn_bt"])), (brow[:, 3, 0:D], rows(T["L2_gnn_bq"])),
                  (WA[:, 0, 0:D], Wt[0:D, :]), (WT2[:, :], Wt[D:2 * D, :])])
        vector_part(lambda v: link(v, v.tensor_copy(Yr, X[:, :, :])))
        layernorm_into(Yr, Yl, Z[:, :, 0:D], row(0, D), row(1, D))
        table2 = nc.dram_tensor("table_l2", [NB * P, D], f32).ap()
        node_matmul(Yl, D, WA, D, Z, brow[:, 2, 0:D])
        store_table(table2, D)
        loads_of([(WA[:, 0, 0:D], T["L2_gnn_Wq"]), (WR[:, 0, 0:D], T["L2_gnn_Wk"]),
                  (vec[:, 0, 0:1], T["L2_gnn_bk"].rearrange("(a b) -> a b", b=1))])
        node_matmul(Yl, D, WA, D, Yr, brow[:, 3, 0:D])
        transposed_weight(WA[:, 0, 0:D])
        vector_part(lambda v: link(v, v.tensor_copy(WA[:, 0, D:D + 1], vec[:, 0, 0:1])))
        node_matmul(Yr, D, WA, D + 1, QK)

        def clear2(v):
            link(v, v.memset(V[:, :, :], NEG))
            link(v, v.memset(acc[:, :, 0:D + 1], 0.0))
        vector_part(clear2)
        edge_attention(table2, T["edge_attr_128"])
        loads_of([(WA[:, 0, 0:D], T["L2_gnn_Wv"]), (brow[:, 0, 0:D], rows(T["L2_gnn_bv"]))])

        def averages(v):
            r = denominators(v, acc[:, :, D:D + 1], 1)
            link(v, v.tensor_tensor(Yl, acc[:, :, 0:D], r.to_broadcast([P, NB, D]), ALU.mult))
            link(v, v.tensor_tensor(small[:, 1, 0:NB].rearrange("p (b a) -> p b a", a=1), acc[:, :, D:D + 1], r, ALU.mult))
        vector_part(averages)
        node_matmul(Yl, D, WA, D, Z)

        def value_bias(v):
            link(v, v.tensor_tensor(Yl, bc(small[:, 1, 0:NB], 2, D), row(0, D), ALU.mult))
            link(v, v.tensor_tensor(Z[:, :, 0:D], Z[:, :, 0:D], Yl, ALU.add))
        vector_act_vector(value_bias, lambda a: a.activation(Yl, Z[:, :, 0:D], ACT.Gelu), None)
        vector_part(lambda v: link(v, v.tensor_tensor(Yl, Yl, X[:, :, :], ALU.add)))
        add_norm(Yl)
        if stop == "l2":
            return finish(X)

        loads_of([(WR[:, 0, 0:D], T["L3_gnn_W1"]), (brow[:, 0, 0:D], rows(T["L3_gnn_b1"])),
                  (brow[:, 1, 0:D], rows(T["L3_gnn_b2"]))])
        transposed_weight(WA[:, 0, 0:D])
        node_matmul(X[:, :, :], D, WA, D, Z, brow[:, 0, 0:D])
        table3 = nc.dram_tensor("table_l3", [NB * P, D], f32).ap()

        def relu(v, dst):
            link(v, v.tensor_scalar(dst, dst, 0.0, None, ALU.max))

        def messages(v):
            relu(v, Z[:, :, 0:D])
            link(v, v.memset(acc[:, :, 0:D], 0.0))
        vector_part(messages)
        store_table(table3, D)
        edge_sums(table3)
        loads_of([(WR[:, 0, 0:D], T["L3_gnn_W2"])])
        transposed_weight(WA[:, 0, 0:D])
        vector_part(lambda v: link(v, v.tensor_tensor(Yl, acc[:, :, 0:D], X[:, :, :], ALU.add)))
        node_matmul(Yl, D, WA, D, Yr, brow[:, 1, 0:D])
        vector_part(lambda v: relu(v, Yr))
        add_norm(Yr)
        finish(X)


def kernel(**inputs):
    import numpy as _np
    import concourse.bacc as _bacc
    from concourse import mybir as _mybir
    from concourse.bass_utils import run_bass_kernel_spmd as _run

    nc = _bacc.Bacc("TRN2", target_bir_lowering=False, num_devices=1)
    arrays, T = {}, {}
    for name, a in inputs.items():
        a = _np.ascontiguousarray(a)
        arrays[f"in_{name}"] = a
        T[name] = nc.dram_tensor(f"in_{name}", a.shape, _mybir.dt.from_np(a.dtype), kind="ExternalInput").ap()
    out = nc.dram_tensor("out_0", (N, D), f32, kind="ExternalOutput").ap()
    gnn(nc, T, out)
    r = _run(nc, [arrays], core_ids=[0])
    return r.results[0]["out_0"]
```
